# Optimizing a Trainium2 kernel written in Bass

```python
import numpy as np
import jax
import jax.numpy as jnp

def _softmax(x, axis=-1):
    return jax.nn.softmax(x, axis=axis)

def _gelu(x):
    return jax.nn.gelu(x, approximate=True)

def _silu(x):
    return jax.nn.silu(x)

def _sigmoid(x):
    return jax.nn.sigmoid(x)

def _layernorm(x, axis=-1, eps=1e-05):
    m = jnp.mean(x, axis=axis, keepdims=True)
    v = jnp.var(x, axis=axis, keepdims=True)
    return (x - m) / jnp.sqrt(v + eps)

def _scatter_add(tgt, idx, src, axis=0):
    return tgt.at[idx].add(src)

def _segment_sum(src, seg, n):
    return jax.ops.segment_sum(src, seg, n)
kernel_name = 'mk_hybrid_d1_jaxref_r8_0e3858'

def setup_inputs(seed: int=0):
    np.random.seed(seed)
    _w = jnp.asarray

    def _L0_attn_a_setup():
        import jax, jax.numpy as jnp
        import numpy as np
        EMBED_DIM = 128
        NUM_HEADS = 16
        HEAD_DIM = EMBED_DIM // NUM_HEADS
        CHUNK_SIZE = 10
        LEFT_CONTEXT = 25
        RIGHT_CONTEXT = 0
        NEG_INF = -1e+30

        def chunk_attention_mask(seq_len: int) -> jnp.ndarray:
            i = jnp.arange(seq_len)[:, None]
            j = jnp.arange(seq_len)[None, :]
            chunk_start = i // CHUNK_SIZE * CHUNK_SIZE
            chunk_end = jnp.minimum(chunk_start + CHUNK_SIZE, seq_len)
            in_chunk = (j >= chunk_start) & (j < chunk_end)
            in_left = (j >= i - LEFT_CONTEXT) & (j < chunk_start)
            in_right = (j >= chunk_end) & (j < jnp.minimum(seq_len, i + RIGHT_CONTEXT + 1))
            allowed = in_chunk | in_left | in_right
            return jnp.where(allowed, 0.0, NEG_INF).astype(jnp.float32)
        key = jax.random.key(seed)
        ks = jax.random.split(key, 9)
        B, S, E = (2, 256, EMBED_DIM)
        s = 1.0 / np.sqrt(E)
        return {'hidden_states': jax.random.normal(ks[0], (B, S, E), jnp.float32), 'Wq': jax.random.normal(ks[1], (E, E), jnp.float32) * s, 'bq': jax.random.normal(ks[2], (E,), jnp.float32) * 0.02, 'Wk': jax.random.normal(ks[3], (E, E), jnp.float32) * s, 'bk': jax.random.normal(ks[4], (E,), jnp.float32) * 0.02, 'Wv': jax.random.normal(ks[5], (E, E), jnp.float32) * s, 'bv': jax.random.normal(ks[6], (E,), jnp.float32) * 0.02, 'Wo': jax.random.normal(ks[7], (E, E), jnp.float32) * s, 'bo': jax.random.normal(ks[8], (E,), jnp.float32) * 0.02}
    _L0_attn_a_in = _L0_attn_a_setup()

    def _L0_attn_b_setup():
        import jax, jax.numpy as jnp
        import numpy as np
        N_HEADS = 16
        key = jax.random.key(seed)
        ks = jax.random.split(key, 9)
        B, S, E = (2, 256, 128)
        s = 1.0 / np.sqrt(E)
        return {'x': jax.random.normal(ks[0], (B, S, E), jnp.float32), 'Wq': jax.random.normal(ks[1], (E, E), jnp.float32) * s, 'bq': jax.random.normal(ks[2], (E,), jnp.float32) * 0.01, 'Wk': jax.random.normal(ks[3], (E, E), jnp.float32) * s, 'bk': jax.random.normal(ks[4], (E,), jnp.float32) * 0.01, 'Wv': jax.random.normal(ks[5], (E, E), jnp.float32) * s, 'bv': jax.random.normal(ks[6], (E,), jnp.float32) * 0.01, 'Wo': jax.random.normal(ks[7], (E, E), jnp.float32) * s, 'bo': jax.random.normal(ks[8], (E,), jnp.float32) * 0.01}
    _L0_attn_b_in = _L0_attn_b_setup()

    def _L0_ffn_setup():
        import jax, jax.numpy as jnp
        import numpy as np
        N_EXPERTS = 32
        TOP_K = 8
        N_GROUP = 4
        TOPK_GROUP = 2
        ROUTED_SCALING = 2.5

        def _gate(x, gate_w, gate_bias):
            T, E = (x.shape[0], gate_w.shape[0])
            logits = jnp.einsum('th,eh->te', x, gate_w)
            scores = jax.nn.sigmoid(logits)
            scores_choice = scores + gate_bias[None, :]
            grp = scores_choice.reshape(T, N_GROUP, E // N_GROUP)
            top2, _ = jax.lax.top_k(grp, 2)
            group_scores = top2.sum(-1)
            _, grp_idx = jax.lax.top_k(group_scores, TOPK_GROUP)
            group_mask = jax.nn.one_hot(grp_idx, N_GROUP, dtype=scores.dtype).sum(1)
            expert_mask = jnp.repeat(group_mask, E // N_GROUP, axis=1)
            masked = jnp.where(expert_mask > 0, scores_choice, 0.0)
            _, topk_idx = jax.lax.top_k(masked, TOP_K)
            topk_w = jnp.take_along_axis(scores, topk_idx, axis=1)
            topk_w = topk_w / (topk_w.sum(-1, keepdims=True) + 1e-20)
            topk_w = topk_w * ROUTED_SCALING
            return (topk_idx, topk_w)

        def _mlp(x, wg, wu, wd):
            return jnp.einsum('...i,hi->...h', jax.nn.silu(jnp.einsum('...h,ih->...i', x, wg)) * jnp.einsum('...h,ih->...i', x, wu), wd)
        key = jax.random.key(seed)
        ks = jax.random.split(key, 9)
        B, S, H, I = (2, 64, 128, 64)
        w = 0.02
        return {'hidden_states': jax.random.normal(ks[0], (B, S, H), jnp.float32), 'gate_w': jax.random.normal(ks[1], (N_EXPERTS, H), jnp.float32) * w, 'gate_bias': jax.random.normal(ks[2], (N_EXPERTS,), jnp.float32) * w, 'expert_gate': jax.random.normal(ks[3], (N_EXPERTS, I, H), jnp.float32) * w, 'expert_up': jax.random.normal(ks[4], (N_EXPERTS, I, H), jnp.float32) * w, 'expert_down': jax.random.normal(ks[5], (N_EXPERTS, H, I), jnp.float32) * w, 'shared_gate': jax.random.normal(ks[6], (2 * I, H), jnp.float32) * w, 'shared_up': jax.random.normal(ks[7], (2 * I, H), jnp.float32) * w, 'shared_down': jax.random.normal(ks[8], (H, 2 * I), jnp.float32) * w}
    _L0_ffn_in = _L0_ffn_setup()
    _d = {'L0_attn_a_hidden_states': _L0_attn_a_in['hidden_states'], 'L0_attn_a_Wq': _L0_attn_a_in['Wq'], 'L0_attn_a_bq': _L0_attn_a_in['bq'], 'L0_attn_a_Wk': _L0_attn_a_in['Wk'], 'L0_attn_a_bk': _L0_attn_a_in['bk'], 'L0_attn_a_Wv': _L0_attn_a_in['Wv'], 'L0_attn_a_bv': _L0_attn_a_in['bv'], 'L0_attn_a_Wo': _L0_attn_a_in['Wo'], 'L0_attn_a_bo': _L0_attn_a_in['bo'], 'L0_attn_b_Wq': _L0_attn_b_in['Wq'], 'L0_attn_b_bq': _L0_attn_b_in['bq'], 'L0_attn_b_Wk': _L0_attn_b_in['Wk'], 'L0_attn_b_bk': _L0_attn_b_in['bk'], 'L0_attn_b_Wv': _L0_attn_b_in['Wv'], 'L0_attn_b_bv': _L0_attn_b_in['bv'], 'L0_attn_b_Wo': _L0_attn_b_in['Wo'], 'L0_attn_b_bo': _L0_attn_b_in['bo'], 'L0_ffn_gate_w': _L0_ffn_in['gate_w'], 'L0_ffn_gate_bias': _L0_ffn_in['gate_bias'], 'L0_ffn_expert_gate': _L0_ffn_in['expert_gate'], 'L0_ffn_expert_up': _L0_ffn_in['expert_up'], 'L0_ffn_expert_down': _L0_ffn_in['expert_down'], 'L0_ffn_shared_gate': _L0_ffn_in['shared_gate'], 'L0_ffn_shared_up': _L0_ffn_in['shared_up'], 'L0_ffn_shared_down': _L0_ffn_in['shared_down']}
    _x0 = _d['L0_attn_a_hidden_states']
    _d['L0_attn_a_hidden_states'] = jax.random.normal(jax.random.fold_in(jax.random.key(seed), 1), (4, 1024, 128), dtype=_x0.dtype)
    del _x0
    return _d

def reference(L0_attn_a_hidden_states, L0_attn_a_Wq, L0_attn_a_bq, L0_attn_a_Wk, L0_attn_a_bk, L0_attn_a_Wv, L0_attn_a_bv, L0_attn_a_Wo, L0_attn_a_bo, L0_attn_b_Wq, L0_attn_b_bq, L0_attn_b_Wk, L0_attn_b_bk, L0_attn_b_Wv, L0_attn_b_bv, L0_attn_b_Wo, L0_attn_b_bo, L0_ffn_gate_w, L0_ffn_gate_bias, L0_ffn_expert_gate, L0_ffn_expert_up, L0_ffn_expert_down, L0_ffn_shared_gate, L0_ffn_shared_up, L0_ffn_shared_down):

    def _L0_attn_a_ref(hidden_states, Wq, bq, Wk, bk, Wv, bv, Wo, bo):
        import jax, jax.numpy as jnp
        import numpy as np
        EMBED_DIM = 128
        NUM_HEADS = 16
        HEAD_DIM = EMBED_DIM // NUM_HEADS
        CHUNK_SIZE = 10
        LEFT_CONTEXT = 25
        RIGHT_CONTEXT = 0
        NEG_INF = -1e+30

        def chunk_attention_mask(seq_len: int) -> jnp.ndarray:
            i = jnp.arange(seq_len)[:, None]
            j = jnp.arange(seq_len)[None, :]
            chunk_start = i // CHUNK_SIZE * CHUNK_SIZE
            chunk_end = jnp.minimum(chunk_start + CHUNK_SIZE, seq_len)
            in_chunk = (j >= chunk_start) & (j < chunk_end)
            in_left = (j >= i - LEFT_CONTEXT) & (j < chunk_start)
            in_right = (j >= chunk_end) & (j < jnp.minimum(seq_len, i + RIGHT_CONTEXT + 1))
            allowed = in_chunk | in_left | in_right
            return jnp.where(allowed, 0.0, NEG_INF).astype(jnp.float32)
        B, S, E = hidden_states.shape
        H, D = (NUM_HEADS, HEAD_DIM)
        scaling = D ** (-0.5)

        def proj(x, W, b):
            y = jnp.einsum('bse,fe->bsf', x, W) + b
            return y.reshape(B, S, H, D).transpose(0, 2, 1, 3)
        q = proj(hidden_states, Wq, bq) * scaling
        k = proj(hidden_states, Wk, bk)
        v = proj(hidden_states, Wv, bv)
        scores = jnp.einsum('bhsd,bhtd->bhst', q, k)
        scores = scores + chunk_attention_mask(S)[None, None]
        probs = jax.nn.softmax(scores, axis=-1)
        out = jnp.einsum('bhst,bhtd->bhsd', probs, v)
        out = out.transpose(0, 2, 1, 3).reshape(B, S, E)
        out = jnp.einsum('bse,fe->bsf', out, Wo) + bo
        return out

    def _L0_attn_b_ref(x, Wq, bq, Wk, bk, Wv, bv, Wo, bo):
        import jax, jax.numpy as jnp
        import numpy as np
        N_HEADS = 16
        B, S, E = x.shape
        H = N_HEADS
        D = E // H
        q = (x @ Wq.T + bq).reshape(B, S, H, D)
        k = (x @ Wk.T + bk).reshape(B, S, H, D)
        v = (x @ Wv.T + bv).reshape(B, S, H, D)
        scores = jnp.einsum('bqnd,bknd->bnqk', q, k) / jnp.sqrt(jnp.float32(D))
        attn = jax.nn.softmax(scores, axis=1)
        out = jnp.einsum('bnqk,bknd->bnqd', attn, v)
        out = out.transpose(0, 2, 1, 3).reshape(B, S, E)
        return out @ Wo.T + bo

    def _L0_ffn_ref(hidden_states, gate_w, gate_bias, expert_gate, expert_up, expert_down, shared_gate, shared_up, shared_down):
        import jax, jax.numpy as jnp
        import numpy as np
        N_EXPERTS = 32
        TOP_K = 8
        N_GROUP = 4
        TOPK_GROUP = 2
        ROUTED_SCALING = 2.5

        def _gate(x, gate_w, gate_bias):
            T, E = (x.shape[0], gate_w.shape[0])
            logits = jnp.einsum('th,eh->te', x, gate_w)
            scores = jax.nn.sigmoid(logits)
            scores_choice = scores + gate_bias[None, :]
            grp = scores_choice.reshape(T, N_GROUP, E // N_GROUP)
            top2, _ = jax.lax.top_k(grp, 2)
            group_scores = top2.sum(-1)
            _, grp_idx = jax.lax.top_k(group_scores, TOPK_GROUP)
            group_mask = jax.nn.one_hot(grp_idx, N_GROUP, dtype=scores.dtype).sum(1)
            expert_mask = jnp.repeat(group_mask, E // N_GROUP, axis=1)
            masked = jnp.where(expert_mask > 0, scores_choice, 0.0)
            _, topk_idx = jax.lax.top_k(masked, TOP_K)
            topk_w = jnp.take_along_axis(scores, topk_idx, axis=1)
            topk_w = topk_w / (topk_w.sum(-1, keepdims=True) + 1e-20)
            topk_w = topk_w * ROUTED_SCALING
            return (topk_idx, topk_w)

        def _mlp(x, wg, wu, wd):
            return jnp.einsum('...i,hi->...h', jax.nn.silu(jnp.einsum('...h,ih->...i', x, wg)) * jnp.einsum('...h,ih->...i', x, wu), wd)
        orig_shape = hidden_states.shape
        H = orig_shape[-1]
        residuals = hidden_states
        x = hidden_states.reshape(-1, H)
        topk_idx, topk_w = _gate(x, gate_w, gate_bias)
        g = jnp.einsum('th,eih->eti', x, expert_gate)
        u = jnp.einsum('th,eih->eti', x, expert_up)
        outs = jnp.einsum('eti,ehi->eth', jax.nn.silu(g) * u, expert_down)
        outs_t = jnp.transpose(outs, (1, 0, 2))
        gathered = jnp.take_along_axis(outs_t, topk_idx[:, :, None], axis=1)
        final = (gathered * topk_w[:, :, None]).sum(1)
        shared = _mlp(residuals, shared_gate, shared_up, shared_down)
        return final.reshape(orig_shape) + shared
    x = L0_attn_a_hidden_states
    x = x + _L0_attn_a_ref(_layernorm(x, axis=-1), L0_attn_a_Wq, L0_attn_a_bq, L0_attn_a_Wk, L0_attn_a_bk, L0_attn_a_Wv, L0_attn_a_bv, L0_attn_a_Wo, L0_attn_a_bo)
    x = x + _L0_ffn_ref(_layernorm(x, axis=-1), L0_ffn_gate_w, L0_ffn_gate_bias, L0_ffn_expert_gate, L0_ffn_expert_up, L0_ffn_expert_down, L0_ffn_shared_gate, L0_ffn_shared_up, L0_ffn_shared_down)
    x = x + _L0_attn_b_ref(_layernorm(x, axis=-1), L0_attn_b_Wq, L0_attn_b_bq, L0_attn_b_Wk, L0_attn_b_bk, L0_attn_b_Wv, L0_attn_b_bv, L0_attn_b_Wo, L0_attn_b_bo)
    x = x + _L0_ffn_ref(_layernorm(x, axis=-1), L0_ffn_gate_w, L0_ffn_gate_bias, L0_ffn_expert_gate, L0_ffn_expert_up, L0_ffn_expert_down, L0_ffn_shared_gate, L0_ffn_shared_up, L0_ffn_shared_down)
    return x

_drawn_inputs = setup_inputs


def setup_inputs(seed=0):
    import zlib

    import numpy as np

    out = dict(_drawn_inputs(seed))
    spreads = {}
    factors = {'L0_attn_a_bq': 3.86,
     'L0_attn_a_bk': 64.0,
     'L0_attn_b_bq': 6.746,
     'L0_attn_b_bk': 6.889,
     'L0_attn_b_bo': 21.548,
     'L0_ffn_gate_w': 8.0,
     'L0_ffn_gate_bias': 8.0,
     'L0_ffn_expert_gate': 8.0,
     'L0_ffn_expert_up': 8.0,
     'L0_ffn_expert_down': 8.0,
     'L0_ffn_shared_gate': 7.723,
     'L0_ffn_shared_up': 7.866,
     'L0_ffn_shared_down': 7.821}
    for name, (base, spread) in spreads.items():
        noise = np.random.default_rng([zlib.crc32(name.encode()), seed]).standard_normal(out[name].shape)
        drawn = base * np.exp(spread * noise) if base else spread * noise
        out[name] = jnp.asarray(drawn.astype(out[name].dtype))
    for name, factor in factors.items():
        out[name] = (out[name] * factor).astype(out[name].dtype)
    return out
```

```python
from contextlib import ExitStack

import numpy as np

import concourse.bass as bass
from concourse import mybir

F32 = mybir.dt.float32
F16 = mybir.dt.float16
BF16 = mybir.dt.bfloat16
ALU = mybir.AluOpType
ACT = mybir.ActivationFunctionType
AX = mybir.AxisListType

P = 128
B, S, E = 4, 1024, 128
T = B * S
NT = T // P
BT = S // P
NH, D = 16, 8
NG, GH = 4, 4
BLK = 512
NBLK = T // BLK
TB = BLK // P
SCALE = float(D) ** -0.5
EPS = 1e-5

CHUNK, LEFT = 10, 25
QT = 100
KW = QT + LEFT
NQT = -(-S // QT)
QPAD = NQT * QT
KPAD = QPAD + LEFT
HH = NH // 2
VA = D + 1

QS = 64
VSLOT = 32
NEXP, INTER = 32, 64
NPAIR = NEXP // 2
EGRP, EPG = 4, 8
TOPG = 2
ROUTED = 2.5
BIG = 1e30
ONE = 1


def tile_at(t, i):
    return t[:, bass.ds(i, 1), :].rearrange("p a e -> p (a e)")


class Chain:

    def __init__(self, eng, sem, base=0):
        self.eng, self.sem, self.base, self.n = eng, sem, base, 0

    def link(self, ins):
        self.n += 1
        ins.then_inc(self.sem, 1)
        self.eng.wait_ge(self.sem, ONE + self.base + self.n)


class Mem:

    def __init__(self, nc, stage):
        self.nc, self.stage, self.ctx, self.sems = nc, stage, ExitStack(), []

    def __enter__(self):
        return self

    def __exit__(self, *exc):
        return self.ctx.__exit__(*exc)

    def sb(self, name, shape, dt=F32):
        return self.ctx.enter_context(self.nc.sbuf_tensor(f"{self.stage}_{name}", shape, dt))

    def ps(self, name, shape, dt=F32):
        return self.ctx.enter_context(self.nc.psum_tensor(f"{self.stage}_{name}", shape, dt))

    def sem(self, name, by=None, credits=0):
        s = self.ctx.enter_context(self.nc.semaphore(f"{self.stage}_{name}"))
        if by:
            self.sems.append((s, by, credits))
        return s

    def start(self, eng, name):
        for s, by, credits in self.sems:
            if by == name:
                eng.sem_inc(s, ONE + credits)


def load_all(nc, pairs, x, x_dram):
    with Mem(nc, "load") as m:
        loaded = m.sem("loaded")
        block = m.ctx.enter_context(nc.Block())

        @block.sync
        def _(sp):
            sp.dma_start(x[:, :, :], x_dram.rearrange("b (t p) e -> p (b t) e", p=P)).then_inc(loaded, 16)
            for dst, src in pairs:
                sp.dma_start(dst, src).then_inc(loaded, 16)
            sp.wait_ge(loaded, 16 * (1 + len(pairs)))


def layernorm_transposed(nc, stage, c, x, xnT, scores=None):
    with Mem(nc, stage) as m:
        stats = m.sb("stats", [P, TB, 6])
        mv = m.sb("mv", [P, NT, 2])
        mvb = m.sb("mvb", [P, TB, 2])
        std = m.sb("std", [P, NT])
        rstd = m.sb("rstd", [P, NT])
        xn = m.sb("xn", [P, 2, TB, E])
        xs = m.sb("xs", [P, 2, BLK])
        turned = m.ps("turned", [P, 2, BLK])
        logits = m.ps("logits", [P, 2, BLK])
        chain, var_ready, std_ready = m.sem("chain", "dve"), m.sem("var_ready", "dve"), m.sem("std_ready", "act")
        xn_ready, turned_ready, xs_ready, xs_copied = m.sem("xn_ready", "dve"), m.sem("turned_ready", "pe", 1), m.sem("xs_ready", "act", 1), m.sem("xs_copied", "pool", 1)
        logits_ready, logits_read, passed = m.sem("logits_ready", "pe"), m.sem("logits_read", "act", 1), m.sem("passed")
        dve_passed = m.sem("dve_passed")
        block = m.ctx.enter_context(nc.Block())

        @block.vector
        def _(dve):
            m.start(dve, "dve")
            with dve.Fori(0, NBLK) as k:
                ch = Chain(dve, chain, k * 3)
                for j in range(TB):
                    last = dve.bn_stats(stats[:, j, :], tile_at(x, k * TB + j))
                ch.link(last)
                dve.sem_inc(dve_passed, 1)
                for j in range(TB):
                    last = dve.bn_aggr(mvb[:, j, :], stats[:, j, :])
                ch.link(last)
                ch.link(dve.tensor_copy(mv[:, bass.ds(k * TB, TB), :], mvb[:, :, :]))
            dve.tensor_scalar(std[:, :], mv[:, :, 1], EPS, None, ALU.add).then_inc(var_ready, 1)
            dve.wait_ge(std_ready, ONE + 1)
            ch = Chain(dve, chain, 3 * NBLK)
            ch.link(dve.reciprocal(rstd[:, :], std[:, :]))
            with dve.Fori(0, NBLK // 2) as pair:
                k = pair * 2
                for u in range(2):
                    dve.wait_ge(turned_ready, ONE + k + u)
                    for j in range(TB):
                        t = k * TB + (u * TB + j)
                        last = dve.tensor_scalar(xn[:, u, j, :], tile_at(x, t), tile_at(mv, t)[:, 0:1], rstd[:, bass.ds(t, 1)], ALU.subtract, ALU.mult)
                    last.then_inc(xn_ready, 1)

        @block.tensor
        def _(pe):
            m.start(pe, "pe")
            with pe.Fori(0, NBLK // 2) as pair:
                k = pair * 2
                for u in range(2):
                    pe.wait_ge(xn_ready, ONE + k + u + 1)
                    pe.wait_ge(xs_ready, ONE + k + u)
                    for j in range(TB):
                        last = pe.transpose(turned[:, u, j * P:(j + 1) * P], xn[:, u, j, :], c["ident"][:, :])
                    last.then_inc(turned_ready, 1)
                    if scores is not None:
                        pe.wait_ge(xs_ready, ONE + k + u + 2)
                        pe.wait_ge(logits_read, ONE + k + u)
                        for j in range(TB):
                            last = pe.matmul(logits[:, u, j * NEXP:(j + 1) * NEXP], xs[:, u, j * P:(j + 1) * P],
                                             c["gate_w"][:, :], start=(j == 0), stop=True, skip_group_check=True)
                        last.then_inc(logits_ready, 1)

        @block.scalar
        def _(act):
            m.start(act, "act")
            act.wait_ge(var_ready, ONE + 1)
            act.activation(std[:, :], std[:, :], ACT.Sqrt).then_inc(std_ready, 1)
            with act.Fori(0, NBLK // 2) as pair:
                k = pair * 2
                for u in range(2):
                    act.wait_ge(turned_ready, ONE + k + u + 2)
                    act.wait_ge(xs_copied, ONE + k + u)
                    act.activation(xs[:, u, :], turned[:, u, :], ACT.Copy).then_inc(xs_ready, 1)
                    if scores is not None:
                        act.wait_ge(logits_ready, ONE + k + u + 1)
                        act.activation(scores[:, bass.ds(k * TB + u * TB, TB), :],
                                       logits[:, u, 0:TB * NEXP].rearrange("p (t e) -> p t e", t=TB),
                                       ACT.Sigmoid).then_inc(logits_read, 1)

        @block.gpsimd
        def _(pool):
            m.start(pool, "pool")
            with pool.Fori(0, NBLK // 2) as pair:
                k = pair * 2
                for u in range(2):
                    pool.wait_ge(xs_ready, ONE + k + u + 2)
                    pool.sem_inc(passed, 1)
                    pool.tensor_copy(xnT[:, bass.ds(k * BLK + u * BLK, BLK)], xs[:, u, :]).then_inc(xs_copied, 1)


class Projections:

    UNITS = 2 * NG * (S // BLK)

    def __init__(self, m, c, att, qcols, kcols, koff, banks):
        self.c, self.att, self.koff, self.banks = c, att, koff, banks
        self.full = m.sb("full", [P, 2, BLK])
        self.high = m.sb("high", [P, 2, BLK], F16)
        self.parts = m.sb("parts", [P, 2, BLK], F16)
        self.QB = m.sb("QB", [P, NH, qcols], F16)
        self.KS = m.sb("KS", [P, NG, kcols], F16)
        self.xb = m.sb("xb", [P, kcols])
        self.xb_ready, self.proj_ready, self.full_ready = m.sem("xb_ready", "pool"), m.sem("proj_ready", "pe"), m.sem("full_ready", "act")
        self.passed = m.sem("passed")
        self.high_ready, self.parts_done, self.parts_chain = m.sem("high_ready", "pool"), m.sem("parts_done", "dve"), m.sem("parts_chain", "dve")

    def unit(self, u):
        kind, rest = divmod(u, self.UNITS // 2)
        g, h = divmod(rest, S // BLK)
        return kind, g, h

    def clear_pads(self, pool, sem):
        n = 0
        for t, lo, hi in ((self.xb, 0, self.koff), (self.xb, self.koff + S, self.xb.shape[1])):
            if hi > lo:
                pool.memset(t[:, lo:hi], 0.0).then_inc(sem, 1)
                n += 1
        for lo, hi in ((0, self.koff), (self.koff + S, self.KS.shape[2])):
            if hi > lo:
                pool.memset(self.KS[:, :, lo:hi], 0.0).then_inc(sem, 1)
                n += 1
        if self.QB.shape[2] > S:
            pool.memset(self.QB[:, :, S:], 0.0).then_inc(sem, 1)
            n += 1
        return n

    def on_pe(self, pe, b):
        pe.wait_ge(self.xb_ready, ONE + b + 1)
        for u in range(self.UNITS):
            kind, g, h = self.unit(u)
            w = self.c[self.att + ("WqR" if kind == 0 else "WkR")]
            if u >= 2:
                pe.wait_ge(self.full_ready, ONE + b * self.UNITS + u - 1)
            pe.matmul(self.banks[u % 2], w[:, g, :], self.xb[:, self.koff + h * BLK:self.koff + (h + 1) * BLK],
                      start=True, stop=True).then_inc(self.proj_ready, 1)

    def on_act(self, act, b):
        for u in range(self.UNITS):
            kind, g, h = self.unit(u)
            bias = self.c[self.att + ("bqR" if kind == 0 else "bkR")]
            act.wait_ge(self.proj_ready, ONE + b * self.UNITS + u + 1)
            if u >= 2:
                act.wait_ge(self.parts_done, ONE + b * self.UNITS + u - 1)
            act.activation(self.full[:, u % 2, :], self.banks[u % 2], ACT.Identity,
                           bias=bias[:, g:g + 1]).then_inc(self.full_ready, 1)

    def on_pool(self, pool, b):
        for u in range(self.UNITS):
            pool.wait_ge(self.full_ready, ONE + b * self.UNITS + u + 1)
            pool.sem_inc(self.passed, 1)
            pool.tensor_copy(self.high[:, u % 2, :], self.full[:, u % 2, :]).then_inc(self.high_ready, 1)

    def on_dve(self, dve, b):
        for u in range(self.UNITS):
            kind, g, h = self.unit(u)
            dve.wait_ge(self.high_ready, ONE + b * self.UNITS + u + 1)
            dve.wait_ge(self.parts_done, ONE + b * self.UNITS + u)
            if kind == 0:
                ch = Chain(dve, self.parts_chain, b * (self.UNITS // 2) + u)
                ch.link(dve.scalar_tensor_tensor(self.parts[:, u % 2, :], self.high[:, u % 2, :], self.c["low_q"][:, 0:1],
                                                 self.full[:, u % 2, :], ALU.mult, ALU.add))
                for n4 in range(GH):
                    last = dve.tensor_scalar(self.QB[:, GH * g + n4, h * BLK:(h + 1) * BLK], self.parts[:, u % 2, :],
                                             self.c["head_rows"][:, n4:n4 + 1], None, ALU.mult)
            else:
                last = dve.scalar_tensor_tensor(self.KS[:, g, self.koff + h * BLK:self.koff + (h + 1) * BLK],
                                                self.high[:, u % 2, :], self.c["low_k"][:, 0:1],
                                                self.full[:, u % 2, :], ALU.mult, ALU.add)
            last.then_inc(self.parts_done, 1)


def banded_attention(nc, c, x, xnT):
    with Mem(nc, "band") as m:
        score = m.ps("score", [P, 2, 2, BLK])
        turned = m.ps("turned", [P, 2, BLK])
        outp = m.ps("outp", [P, BLK])
        spare = m.ps("spare", [P, BLK])
        pr = Projections(m, c, "a_", QPAD, KPAD, LEFT, [score[:, 0, 0, :], score[:, 0, 1, :]])
        vw = m.sb("vw", [P, NQT * NH, VA])
        negm = m.sb("negm", [P, 2, HH])
        nmh = m.sb("nmh", [P, 2, HH], BF16)
        nml = m.sb("nml", [P, 2, HH], BF16)
        prob = m.sb("prob", [P, 2, HH, KW])
        probT = m.sb("probT", [P, 2, HH, QT])
        rden = m.sb("rden", [P, NH])
        on = m.sb("on", [P, NH, D])
        attT = m.sb("attT", [P, QPAD])
        cleared, v_ready, v_done = m.sem("cleared", "pool"), m.sem("v_ready", "pe"), m.sem("v_done", "dve")
        score_ready, shift_ready, shifted = m.sem("score_ready", "pe"), m.sem("shift_ready", "dve"), m.sem("shifted", "pe")
        prob_ready, turned_ready, probT_ready = m.sem("prob_ready", "act"), m.sem("turned_ready", "pe"), m.sem("probT_ready", "act")
        out_ready, on_ready, onT_ready, attT_ready = m.sem("out_ready", "pe"), m.sem("on_ready", "dve"), m.sem("onT_ready", "pe"), m.sem("attT_ready", "act")
        proj_ready, added, chain, passed = m.sem("proj_o_ready", "pe"), m.sem("added", "dve"), m.sem("chain", "dve"), m.sem("pe_passed")
        CPT = 5
        block = m.ctx.enter_context(nc.Block())
        NCLEAR = 6

        @block.gpsimd
        def _(pool):
            m.start(pool, "pool")
            n = pr.clear_pads(pool, cleared)
            pool.memset(vw[:, :, D:VA], 1.0).then_inc(cleared, 1)
            assert n + 1 == NCLEAR
            with pool.Fori(0, B) as b:
                pool.wait_ge(v_ready, ONE + b * NQT)
                pool.sem_inc(pr.passed, 1)
                pool.tensor_copy(pr.xb[:, LEFT:LEFT + S], xnT[:, bass.ds(b * S, S)]).then_inc(pr.xb_ready, 1)
                pr.on_pool(pool, b)

        @block.tensor
        def _(pe):
            m.start(pe, "pe")
            pe.wait_ge(cleared, ONE + NCLEAR)
            with pe.Fori(0, B) as b:
                pr.on_pe(pe, b)
                for w in range(NQT):
                    if w >= 2:
                        pe.wait_ge(v_done, ONE + b * NQT + w - 1)
                    pe.matmul(score[0:KW, 1, w % 2, 0:E], pr.xb[:, w * QT:w * QT + KW], c["a_WvT"][:, :],
                              start=True, stop=True).then_inc(v_ready, 1)
                pe.wait_ge(pr.parts_done, ONE + (b + 1) * pr.UNITS)
                pe.wait_ge(v_done, ONE + (b + 1) * NQT)
                pe.sem_inc(passed, 1)
                with pe.Fori(0, NQT) as t:
                    step = b * (2 * NQT) + t * 2
                    tile = b * NQT + t
                    for h in range(2):
                        for j in range(HH):
                            n = HH * h + j
                            pe.matmul(score[0:QT, h, j // GH, (j % GH) * KW:(j % GH + 1) * KW],
                                      pr.QB[:, n, bass.ds(t * QT, QT)], pr.KS[:, n // GH, bass.ds(t * QT, KW)],
                                      start=(j % GH == 0), stop=False, skip_group_check=True)
                        for k in range(2):
                            last = pe.matmul(score[0:QT, h, k, 0:GH * KW].rearrange("p (a w) -> p a w", a=GH), c["identb"][0:QT, 0:QT],
                                             tile_at(c["band"], t)[0:QT, :][:, None, :].broadcast_to([QT, GH, KW]),
                                             start=False, stop=False, skip_group_check=True)
                        last.then_inc(score_ready, 1)
                    for h in range(2):
                        pe.wait_ge(shift_ready, ONE + step + h + 1)
                        for k in range(2):
                            for part in (nmh, nml):
                                last = pe.matmul(score[0:QT, h, k, 0:GH * KW].rearrange("p (a w) -> p a w", a=GH), c["identb"][0:QT, 0:QT],
                                                 part[0:QT, h, k * GH:(k + 1) * GH][:, :, None].broadcast_to([QT, GH, KW]),
                                                 start=False, stop=(part is nml), skip_group_check=True)
                        last.then_inc(shifted, 1)
                    for h in range(2):
                        pe.wait_ge(prob_ready, ONE + step + h + 1)
                        pe.wait_ge(probT_ready, ONE + step + h)
                        for j in range(HH):
                            last = pe.transpose(turned[0:KW, j // GH, (j % GH) * QT:(j % GH + 1) * QT],
                                                prob[0:QT, h, j, :], c["ident"][0:QT, 0:QT])
                        last.then_inc(turned_ready, 1)
                    for h in range(2):
                        pe.wait_ge(probT_ready, ONE + step + h + 1)
                        if h == 0:
                            pe.wait_ge(attT_ready, ONE + tile)
                        for j in range(HH):
                            n = HH * h + j
                            last = pe.matmul(outp[0:QT, n * VA:(n + 1) * VA], probT[0:KW, h, j, :], tile_at(vw, t * NH + n)[0:KW, :],
                                             start=(n == 0), stop=True, skip_group_check=True)
                    last.then_inc(out_ready, 1)
                    pe.wait_ge(on_ready, ONE + tile + 1)
                    pe.transpose(outp[:, 256:256 + QT], on[0:QT, :, :].rearrange("p n d -> p (n d)"),
                                 c["ident"][0:QT, 0:QT]).then_inc(onT_ready, 1)
                pe.wait_ge(attT_ready, ONE + (b + 1) * NQT)
                for j in range(BT):
                    if j >= 1:
                        pe.wait_ge(added, ONE + b * BT + j)
                    pe.matmul(spare[:, 0:E], attT[:, j * P:(j + 1) * P], c["a_WoT"][:, :], start=True, stop=False)
                    pe.matmul(spare[:, 0:E], c["ones"][0:1, :], c["a_bo"][0:1, :], start=False, stop=True)\
                        .then_inc(proj_ready, 1)
                pe.wait_ge(added, ONE + (b + 1) * BT)

        @block.scalar
        def _(act):
            m.start(act, "act")
            with act.Fori(0, B) as b:
                pr.on_act(act, b)
                with act.Fori(0, NQT) as t:
                    step = b * (2 * NQT) + t * 2
                    tile = b * NQT + t
                    for h in range(2):
                        act.wait_ge(shifted, ONE + step + h + 1)
                        act.wait_ge(turned_ready, ONE + step)
                        act.activation(prob[0:QT, h, :, :].rearrange("p (k a) w -> p k (a w)", k=2),
                                       score[0:QT, h, :, 0:GH * KW], ACT.Exp, scale=SCALE).then_inc(prob_ready, 1)
                    for h in range(2):
                        act.wait_ge(turned_ready, ONE + step + h + 1)
                        act.wait_ge(out_ready, ONE + tile)
                        act.activation(probT[0:KW, h, :, :].rearrange("p (k a) q -> p k (a q)", k=2),
                                       turned[0:KW, :, 0:GH * QT], ACT.Copy).then_inc(probT_ready, 1)
                    act.wait_ge(onT_ready, ONE + tile + 1)
                    act.wait_ge(proj_ready, ONE + b * BT)
                    act.activation(attT[:, bass.ds(t * QT, QT)], outp[:, 256:256 + QT], ACT.Copy).then_inc(attT_ready, 1)

        @block.vector
        def _(dve):
            m.start(dve, "dve")
            with dve.Fori(0, B) as b:
                dve.wait_ge(onT_ready, ONE + b * NQT)
                pr.on_dve(dve, b)
                for w in range(NQT):
                    dve.wait_ge(v_ready, ONE + b * NQT + w + 1)
                    dve.tensor_tensor(vw[0:KW, w * NH:(w + 1) * NH, 0:D], score[0:KW, 1, w % 2, 0:E].rearrange("p (n d) -> p n d", n=NH),
                                      c["a_bv"][0:KW, :].rearrange("p (n d) -> p n d", n=NH), ALU.add).then_inc(v_done, 1)
                with dve.Fori(0, NQT) as t:
                    step = b * (2 * NQT) + t * 2
                    tile = b * NQT + t
                    ch = Chain(dve, chain, tile * CPT)
                    for h in range(2):
                        dve.wait_ge(score_ready, ONE + step + h + 1)
                        dve.wait_ge(shifted, ONE + step)
                        dve.wait_ge(shift_ready, ONE + step + h)
                        ch.link(dve.tensor_reduce(negm[0:QT, h, :].rearrange("p (k a) -> p k a", k=2),
                                                  score[0:QT, h, :, 0:GH * KW].rearrange("p k (a w) -> p k a w", a=GH),
                                                  AX.X, ALU.max, negate=True))
                        ch.link(dve.tensor_copy(nmh[0:QT, h, :], negm[0:QT, h, :]))
                        dve.tensor_tensor(nml[0:QT, h, :], negm[0:QT, h, :], nmh[0:QT, h, :], ALU.subtract)\
                            .then_inc(shift_ready, 1)
                    dve.wait_ge(out_ready, ONE + tile + 1)
                    dve.wait_ge(on_ready, ONE + tile)
                    o = outp[0:QT, 0:NH * VA].rearrange("p (n v) -> p n v", v=VA)
                    ch.link(dve.reciprocal(rden[0:QT, :], o[:, :, D]))
                    dve.wait_ge(onT_ready, ONE + tile)
                    dve.tensor_tensor(on[0:QT, :, :], o[:, :, 0:D], rden[0:QT, :][:, :, None].broadcast_to([QT, NH, D]),
                                      ALU.mult).then_inc(on_ready, 1)
                    assert ch.n == CPT
                for j in range(BT):
                    dve.wait_ge(proj_ready, ONE + b * BT + j + 1)
                    xt = tile_at(x, b * BT + j)
                    dve.tensor_tensor(xt, xt, spare[:, 0:E], ALU.add).then_inc(added, 1)


def head_softmax_attention(nc, c, x, xnT):
    NQ = S // P
    NS = 2 * BT
    STEPS = NQ * NS
    FRONT = STEPS + 1
    with Mem(nc, "head") as m:
        score = m.ps("score", [P, 2, 2, BLK])
        recip = m.ps("recip", [P, 2, BLK])
        outp = m.ps("outp", [P, BLK])
        spare = m.ps("spare", [P, BLK])
        pr = Projections(m, c, "b_", S + P, S, 0, [score[:, 0, 0, :], score[:, 0, 1, :]])
        vs = m.sb("vs", [P, BT, (NH + 1) * VSLOT])
        negm = m.sb("negm", [P, 2, QS])
        nmh = m.sb("nmh", [P, 2, QS], BF16)
        nml = m.sb("nml", [P, 2, QS], BF16)
        ex = m.sb("ex", [P, 2, NH, QS])
        half = m.sb("half", [P, NH // 2, QS])
        den = m.sb("den", [P, 2, QS])
        lnd = m.sb("lnd", [P, 2, QS])
        prob = m.sb("prob", [P, 2, NH, P])
        outT = m.sb("outT", [P, S])
        cleared, v_ready, v_done = m.sem("cleared", "pool"), m.sem("v_ready", "pe"), m.sem("v_done", "dve")
        score_ready, shift_ready, shifted = m.sem("score_ready", "pe"), m.sem("shift_ready", "dve"), m.sem("shifted", "pe")
        ex_ready, den_ready, recip_ready, prob_ready = m.sem("ex_ready", "act"), m.sem("den_ready", "pool"), m.sem("recip_ready", "act", 1), m.sem("prob_ready", "dve", 1)
        av_done, outT_ready = m.sem("av_done", "pe", 1), m.sem("outT_ready", "act")
        proj_ready, added = m.sem("proj_o_ready", "pe"), m.sem("added", "dve")
        chain, act_chain, pool_chain = m.sem("chain", "dve"), m.sem("act_chain", "act"), m.sem("pool_chain", "pool")
        block = m.ctx.enter_context(nc.Block())
        NCLEAR = 2

        def bank(buf, n):
            return score[:, buf, n // (NH // 2), (n % (NH // 2)) * QS:(n % (NH // 2) + 1) * QS]

        @block.gpsimd
        def _(pool):
            m.start(pool, "pool")
            n = pr.clear_pads(pool, cleared)
            pool.memset(vs[:, :, :], 0.0).then_inc(cleared, 1)
            assert n + 1 == NCLEAR
            with pool.Fori(0, B) as b:
                pool.wait_ge(v_ready, ONE + b * BT)
                pool.sem_inc(pr.passed, 1)
                pool.tensor_copy(pr.xb[:, :], xnT[:, bass.ds(b * S, S)]).then_inc(pr.xb_ready, 1)
                pr.on_pool(pool, b)
                with pool.Fori(0, NQ) as q:
                    for s in range(NS):
                        step = b * STEPS + q * NS + s
                        e, hf = ex[:, s % 2, :, :], half[:, :, :]
                        ch = Chain(pool, pool_chain, step * 3)
                        pool.wait_ge(ex_ready, ONE + step + 1)
                        pool.wait_ge(den_ready, ONE + step)
                        pool.wait_ge(recip_ready, ONE + step)
                        ch.link(pool.tensor_tensor(hf, e[:, 0:8, :], e[:, 8:16, :], ALU.add))
                        ch.link(pool.tensor_tensor(hf[:, 0:4, :], hf[:, 0:4, :], hf[:, 4:8, :], ALU.add))
                        ch.link(pool.tensor_tensor(hf[:, 0:2, :], hf[:, 0:2, :], hf[:, 2:4, :], ALU.add))
                        pool.tensor_tensor(den[:, s % 2, :], hf[:, 0, :], hf[:, 1, :], ALU.add).then_inc(den_ready, 1)

        @block.tensor
        def _(pe):
            m.start(pe, "pe")
            pe.wait_ge(cleared, ONE + NCLEAR)

            def scores_of(b, q, s):
                kt, h = divmod(s % NS, 2)
                cols = q * P + (s // NS) * P + h * QS
                for g in range(NG):
                    last = pe.matmul(score[:, s % 2, g // 2, (g % 2) * GH * QS:(g % 2 + 1) * GH * QS].rearrange("p (a w) -> p a w", a=GH),
                                     pr.KS[:, g, kt * P:(kt + 1) * P], pr.QB[:, g * GH:(g + 1) * GH, bass.ds(cols, QS)],
                                     start=(g % 2 == 0), stop=False, skip_group_check=True)
                last.then_inc(score_ready, 1)

            def attend(b, q, kt):
                pe.wait_ge(prob_ready, ONE + b * STEPS + q * NS + (2 * kt + 3))
                if kt == 0:
                    pe.wait_ge(outT_ready, ONE + b * NQ + q)
                for n in range(NH):
                    g, n4 = divmod(n, GH)
                    at = n * VSLOT + VSLOT - D - n4 * D
                    last = pe.matmul(outp[g * 32:(g + 1) * 32, 0:P], vs[:, kt, at:at + 32], prob[:, kt % 2, n, :],
                                     start=(kt == 0 and n4 == 0), stop=(kt == BT - 1 and n4 == GH - 1), skip_group_check=True)
                last.then_inc(av_done, 1)

            with pe.Fori(0, B) as b:
                pe.wait_ge(shift_ready, ONE + b * FRONT)
                pr.on_pe(pe, b)
                for w in range(BT):
                    if w >= 2:
                        pe.wait_ge(v_done, ONE + b * BT + w - 1)
                    pe.matmul(score[:, 1, w % 2, 0:E], pr.xb[:, w * P:(w + 1) * P], c["b_WvT"][:, :],
                              start=True, stop=True).then_inc(v_ready, 1)
                pe.wait_ge(pr.parts_done, ONE + (b + 1) * pr.UNITS)
                pe.wait_ge(v_done, ONE + (b + 1) * BT)
                scores_of(b, 0, 0)
                with pe.Fori(0, NQ) as q:
                    for s in range(NS):
                        step = b * STEPS + q * NS + s
                        front = b * FRONT + q * NS + s
                        pe.wait_ge(ex_ready, ONE + step)
                        scores_of(b, q, s + 1)
                        pe.wait_ge(shift_ready, ONE + front + 1)
                        for k in range(2):
                            for part in (nmh, nml):
                                last = pe.matmul(score[:, s % 2, k, :].rearrange("p (a w) -> p a w", a=NH // 2), c["identb"][:, :],
                                                 part[:, s % 2, :][:, None, :].broadcast_to([P, NH // 2, QS]),
                                                 start=False, stop=(part is nml), skip_group_check=True)
                        last.then_inc(shifted, 1)
                        if s % 2 == 1 and s > 1:
                            attend(b, q, s // 2 - 1)
                    attend(b, q, BT - 1)
                pe.wait_ge(outT_ready, ONE + (b + 1) * NQ)
                for j in range(BT):
                    if j >= 1:
                        pe.wait_ge(added, ONE + b * BT + j)
                    pe.matmul(spare[:, 0:E], outT[:, j * P:(j + 1) * P], c["b_WoT"][:, :], start=True, stop=False)
                    pe.matmul(spare[:, 0:E], c["ones"][0:1, :], c["b_bo"][0:1, :], start=False, stop=True)\
                        .then_inc(proj_ready, 1)
                pe.wait_ge(added, ONE + (b + 1) * BT)

        @block.scalar
        def _(act):
            m.start(act, "act")
            def reciprocal_of(b, q, s, step):
                ch = Chain(act, act_chain, step)
                act.wait_ge(den_ready, ONE + step + 1)
                ch.link(act.activation(lnd[:, s % 2, :], den[:, s % 2, :], ACT.Ln))
                act.activation(recip[:, s % 2, 0:QS], lnd[:, s % 2, :], ACT.Exp, scale=-1.0).then_inc(recip_ready, 1)

            with act.Fori(0, B) as b:
                pr.on_act(act, b)
                with act.Fori(0, NQ) as q:
                    for s in range(NS):
                        step = b * STEPS + q * NS + s
                        act.wait_ge(shifted, ONE + step + 1)
                        act.wait_ge(prob_ready, ONE + step)
                        act.activation(ex[:, s % 2, :, :].rearrange("p (k a) w -> p k (a w)", k=2),
                                       score[:, s % 2, :, :], ACT.Exp, scale=SCALE).then_inc(ex_ready, 1)
                        if s >= 1:
                            reciprocal_of(b, q, s - 1, step - 1)
                    reciprocal_of(b, q, NS - 1, b * STEPS + q * NS + (NS - 1))
                    act.wait_ge(av_done, ONE + (b * NQ + q + 1) * BT + 1)
                    act.wait_ge(proj_ready, ONE + b * BT)
                    act.activation(outT[:, bass.ds(q * P, P)], outp[:, 0:P], ACT.Copy).then_inc(outT_ready, 1)

        @block.vector
        def _(dve):
            m.start(dve, "dve")
            dve.wait_ge(cleared, ONE + NCLEAR)

            def largest(b, q, s, front):
                ch = Chain(dve, chain, front * 2)
                dve.wait_ge(score_ready, ONE + front + 1)
                dve.wait_ge(shift_ready, ONE + front)
                ch.link(dve.tensor_reduce(negm[:, s % 2, :], score[:, s % 2, :, :].rearrange("p k (a w) -> p w k a", a=NH // 2),
                                          AX.XY, ALU.max, negate=True))
                ch.link(dve.tensor_copy(nmh[:, s % 2, :], negm[:, s % 2, :]))
                dve.tensor_tensor(nml[:, s % 2, :], negm[:, s % 2, :], nmh[:, s % 2, :], ALU.subtract).then_inc(shift_ready, 1)

            def weigh(b, q, s, step):
                kt, h = divmod(s, 2)
                dve.wait_ge(recip_ready, ONE + step + 2)
                dve.wait_ge(av_done, ONE + b * (NQ * BT) + q * BT + kt)
                dve.tensor_tensor(prob[:, kt % 2, :, h * QS:(h + 1) * QS], ex[:, s % 2, :, :],
                                  recip[:, s % 2, 0:QS][:, None, :].broadcast_to([P, NH, QS]), ALU.mult).then_inc(prob_ready, 1)

            with dve.Fori(0, B) as b:
                dve.wait_ge(av_done, ONE + b * (NQ * BT) + 1)
                pr.on_dve(dve, b)
                for w in range(BT):
                    dve.wait_ge(v_ready, ONE + b * BT + w + 1)
                    dve.tensor_tensor(vs[:, w, 0:NH * VSLOT].rearrange("p (n s) -> p n s", n=NH)[:, :, VSLOT - D:],
                                      score[:, 1, w % 2, 0:E].rearrange("p (n d) -> p n d", n=NH),
                                      c["b_bv"][:, :].rearrange("p (n d) -> p n d", n=NH), ALU.add).then_inc(v_done, 1)
                largest(b, 0, 0, b * FRONT)
                with dve.Fori(0, NQ) as q:
                    for s in range(NS):
                        step = b * STEPS + q * NS + s
                        largest(b, q, s + 1, b * FRONT + q * NS + (s + 1))
                        if s >= 1:
                            weigh(b, q, s - 1, step - 1)
                    weigh(b, q, NS - 1, b * STEPS + q * NS + (NS - 1))
                for j in range(BT):
                    dve.wait_ge(proj_ready, ONE + b * BT + j + 1)
                    xt = tile_at(x, b * BT + j)
                    dve.tensor_tensor(xt, xt, spare[:, 0:E], ALU.add).then_inc(added, 1)


def route(nc, stage, c, sc, wT):
    with Mem(nc, stage) as m:
        ch_ = m.sb("choice", [P, NT, NEXP])
        ta = m.sb("ta", [P, NT, NEXP])
        tb = m.sb("tb", [P, NT, NEXP])
        g1, g2, gs = m.sb("g1", [P, NT, EGRP]), m.sb("g2", [P, NT, EGRP]), m.sb("gs", [P, NT, EGRP])
        pa, pb = m.sb("pa", [P, NT, EGRP, EGRP]), m.sb("pb", [P, NT, EGRP, EGRP])
        top = m.sb("top", [P, NT, 8])
        tot = m.sb("tot", [P, NT])
        w3 = m.sb("w3", [P, NT, 3 * NEXP], BF16)
        pt = m.ps("pt", [P, 2, BLK])
        chain, w3_ready, pt_ready, pt_read = m.sem("chain", "dve"), m.sem("w3_ready", "dve"), m.sem("pt_ready", "pe"), m.sem("pt_read", "act")
        block = m.ctx.enter_context(nc.Block())

        @block.vector
        def _(dve):
            m.start(dve, "dve")
            L = Chain(dve, chain).link
            bg = c["gate_bias"][:, :][:, None, :].broadcast_to([P, NT, NEXP])
            by_group = lambda a: a[:, :, :].rearrange("p t (g e) -> p t g e", g=EGRP)
            L(dve.tensor_tensor(ch_[:, :, :], sc[:, :, :], bg, ALU.add))
            L(dve.tensor_reduce(g1[:, :, :], by_group(ch_), AX.X, ALU.max))
            for g in range(EGRP):
                last = dve.tensor_tensor(ta[:, :, g * EPG:(g + 1) * EPG], ch_[:, :, g * EPG:(g + 1) * EPG],
                                         g1[:, :, g:g + 1].broadcast_to([P, NT, EPG]), ALU.is_equal)
            L(last)
            L(dve.tensor_reduce(g2[:, :, :], by_group(ta), AX.X, ALU.add))
            L(dve.scalar_tensor_tensor(tb[:, :, :], ta[:, :, :], -BIG, ch_[:, :, :], ALU.mult, ALU.add))
            L(dve.tensor_scalar(g2[:, :, :], g2[:, :, :], 1.5, -BIG, ALU.is_lt, ALU.mult))
            L(dve.tensor_tensor(g2[:, :, :], g2[:, :, :], g1[:, :, :], ALU.add))
            L(dve.tensor_reduce(gs[:, :, :], by_group(tb), AX.X, ALU.max))
            L(dve.tensor_tensor(gs[:, :, :], gs[:, :, :], g2[:, :, :], ALU.max))
            L(dve.tensor_tensor(gs[:, :, :], gs[:, :, :], g1[:, :, :], ALU.add))
            for g in range(EGRP):
                own = gs[:, :, g:g + 1].broadcast_to([P, NT, EGRP])
                dve.tensor_tensor(pa[:, :, g, :], gs[:, :, :], own, ALU.is_ge)
                last = dve.tensor_tensor(pb[:, :, g, :], gs[:, :, :], own, ALU.is_gt)
            L(last)
            for g in range(EGRP):
                last = dve.tensor_tensor(pa[:, :, g, :], pa[:, :, g, :],
                                         c["lower"][:, g * EGRP:(g + 1) * EGRP][:, None, :].broadcast_to([P, NT, EGRP]), ALU.mult)
            L(last)
            L(dve.tensor_tensor(pa[:, :, :, :].rearrange("p t a b -> p (t a b)"), pa[:, :, :, :].rearrange("p t a b -> p (t a b)"),
                                pb[:, :, :, :].rearrange("p t a b -> p (t a b)"), ALU.max))
            L(dve.tensor_reduce(g1[:, :, :], pa[:, :, :, :], AX.X, ALU.add))
            L(dve.tensor_scalar(g1[:, :, :], g1[:, :, :], TOPG - 0.5, None, ALU.is_lt))
            for g in range(EGRP):
                last = dve.tensor_tensor(ta[:, :, g * EPG:(g + 1) * EPG], ch_[:, :, g * EPG:(g + 1) * EPG],
                                         g1[:, :, g:g + 1].broadcast_to([P, NT, EPG]), ALU.mult)
            L(last)
            L(dve.tensor_scalar(ta[:, :, :], ta[:, :, :], 0.0, None, ALU.add))
            for t in range(NT):
                last = dve.max(top[:, t, :], ta[:, t, :])
            L(last)
            for t in range(NT):
                last = dve.match_replace(tb[:, t, :], top[:, t, :], ta[:, t, :], -BIG)
            L(last)
            L(dve.tensor_scalar(tb[:, :, :], tb[:, :, :], -0.5 * BIG, None, ALU.is_lt))
            L(dve.tensor_tensor(ta[:, :, :], sc[:, :, :], tb[:, :, :], ALU.mult))
            L(dve.tensor_reduce(tot[:, :], ta[:, :, :], AX.X, ALU.add))
            L(dve.tensor_scalar(tot[:, :], tot[:, :], 1e-20, None, ALU.add))
            L(dve.reciprocal(tot[:, :], tot[:, :]))
            L(dve.tensor_tensor(ta[:, :, :], ta[:, :, :], tot[:, :][:, :, None].broadcast_to([P, NT, NEXP]), ALU.mult))
            L(dve.tensor_scalar(ta[:, :, :], ta[:, :, :], ROUTED, None, ALU.mult))
            L(dve.tensor_copy(w3[:, :, 0:NEXP], ta[:, :, :]))
            L(dve.tensor_tensor(tb[:, :, :], ta[:, :, :], w3[:, :, 0:NEXP], ALU.subtract))
            L(dve.tensor_copy(w3[:, :, NEXP:2 * NEXP], tb[:, :, :]))
            dve.tensor_tensor(w3[:, :, 2 * NEXP:3 * NEXP], tb[:, :, :], w3[:, :, NEXP:2 * NEXP], ALU.subtract).then_inc(w3_ready, 1)

        @block.tensor
        def _(pe):
            m.start(pe, "pe")
            pe.wait_ge(w3_ready, ONE + 1)
            with pe.Fori(0, NBLK // 2) as pair:
                k = pair * 2
                for u in range(2):
                    pe.wait_ge(pt_read, ONE + k + u)
                    for j in range(TB):
                        last = pe.matmul(pt[0:3 * NEXP, u, j * P:(j + 1) * P], tile_at(w3, k * TB + (u * TB + j)), c["identb"][:, :],
                                         start=(j == 0), stop=True, skip_group_check=True)
                    last.then_inc(pt_ready, 1)

        @block.scalar
        def _(act):
            m.start(act, "act")
            with act.Fori(0, NBLK // 2) as pair:
                k = pair * 2
                for u in range(2):
                    act.wait_ge(pt_ready, ONE + k + u + 1)
                    act.activation(wT[0:3 * NEXP, bass.ds(k * BLK + u * BLK, BLK)], pt[0:3 * NEXP, u, :], ACT.Copy).then_inc(pt_read, 1)


def experts(nc, stage, c, x, xnT, wT):
    NU = NPAIR + 1
    with Mem(nc, stage) as m:
        gate, up, wide = m.ps("gate", [P, 2, BLK]), m.ps("up", [P, 2, BLK]), m.ps("wide", [P, 2, BLK])
        down = m.ps("down", [P, BLK])
        back = m.ps("back", [P, BLK])
        sg, h1, h2 = m.sb("sg", [P, 2, BLK]), m.sb("h1", [P, BLK]), m.sb("h2", [P, 2, BLK])
        dT = m.sb("dT", [P, BLK])
        gate_ready, up_ready, sg_ready, h_ready = m.sem("gate_ready", "pe"), m.sem("up_ready", "pe"), m.sem("sg_ready", "act"), m.sem("h_ready", "dve", 1)
        dT_ready, back_ready, added, chain = m.sem("dT_ready", "act"), m.sem("back_ready", "pe"), m.sem("added", "dve"), m.sem("chain", "dve")
        down_done = m.sem("down_done", "pe", 1)
        block = m.ctx.enter_context(nc.Block())

        @block.tensor
        def _(pe):
            m.start(pe, "pe")
            with pe.Fori(0, NBLK) as k:
                xk = xnT[:, bass.ds(k * BLK, BLK)]

                def down_of(i):
                    pe.wait_ge(h_ready, ONE + k * NU + (i + 2))
                    if i == 0:
                        pe.wait_ge(dT_ready, ONE + k)
                    w = c["Wd"][:, i, :] if i < NPAIR else c["Sd"][:, :]
                    pe.matmul(down[:, :], w, h2[:, i % 2, :], start=(i == 0), stop=(i == NPAIR)).then_inc(down_done, 1)

                for i in range(NU):
                    pe.wait_ge(h_ready, ONE + k * NU + i + (i == 0))
                    gw = c["Wg"][:, i * P:(i + 1) * P] if i < NPAIR else c["Sg"][:, :]
                    uw = c["Wu"][:, i * P:(i + 1) * P] if i < NPAIR else c["Su"][:, :]
                    pe.matmul(gate[:, i % 2, :], gw, xk, start=True, stop=True).then_inc(gate_ready, 1)
                    last = pe.matmul(up[:, i % 2, :], uw, xk, start=True, stop=True)
                    if i < NPAIR:
                        last = pe.matmul(wide[:, i % 2, :], c["pair_rows"][0:3 * NEXP, i, :], wT[0:3 * NEXP, bass.ds(k * BLK, BLK)],
                                         start=True, stop=True)
                    last.then_inc(up_ready, 1)
                    if i >= 1:
                        down_of(i - 1)
                down_of(NPAIR)
                pe.wait_ge(dT_ready, ONE + k + 1)
                pe.wait_ge(added, ONE + k)
                for j in range(TB):
                    last = pe.transpose(back[:, j * P:(j + 1) * P], dT[:, j * P:(j + 1) * P], c["ident"][:, :])
                last.then_inc(back_ready, 1)

        @block.scalar
        def _(act):
            m.start(act, "act")
            with act.Fori(0, NBLK) as k:
                for i in range(NU):
                    act.wait_ge(gate_ready, ONE + k * NU + i + 1)
                    act.wait_ge(h_ready, ONE + k * NU + i + (i == 0))
                    act.activation(sg[:, i % 2, :], gate[:, i % 2, :], ACT.Silu).then_inc(sg_ready, 1)
                act.wait_ge(down_done, ONE + (k + 1) * NU + 1)
                act.wait_ge(back_ready, ONE + k)
                act.activation(dT[:, :], down[:, :], ACT.Copy).then_inc(dT_ready, 1)

        @block.vector
        def _(dve):
            m.start(dve, "dve")
            with dve.Fori(0, NBLK) as k:
                for i in range(NU):
                    ch = Chain(dve, chain, k * (NU - 1) + i)
                    dve.wait_ge(sg_ready, ONE + k * NU + i + 1)
                    dve.wait_ge(up_ready, ONE + k * NU + i + 1)
                    dve.wait_ge(down_done, ONE + k * NU + i + (i == 0))
                    if i < NPAIR:
                        dve.wait_ge(h_ready, ONE + k * NU + i + 1)
                        ch.link(dve.tensor_tensor(h1[:, :], sg[:, i % 2, :], up[:, i % 2, :], ALU.mult))
                        dve.tensor_tensor(h2[:, i % 2, :], h1[:, :], wide[:, i % 2, :], ALU.mult).then_inc(h_ready, 1)
                    else:
                        dve.tensor_tensor(h2[:, i % 2, :], sg[:, i % 2, :], up[:, i % 2, :], ALU.mult).then_inc(h_ready, 1)
                dve.wait_ge(back_ready, ONE + k + 1)
                xt = x[:, bass.ds(k * TB, TB), :]
                dve.tensor_tensor(xt, xt, back[:, :].rearrange("p (t e) -> p t e", t=TB), ALU.add).then_inc(added, 1)


def store_x(nc, x, out):
    with Mem(nc, "store") as m:
        stored = m.sem("stored")
        block = m.ctx.enter_context(nc.Block())

        @block.sync
        def _(sp):
            sp.dma_start(out.rearrange("b (t p) e -> p (b t) e", p=P), x[:, :, :]).then_inc(stored, 16)
            sp.wait_ge(stored, 16)


SHAPES = {
    "ident": ([P, P], F32), "identb": ([P, P], BF16), "ones": ([1, P], F32),
    "band": ([QT, NQT, KW], BF16), "pair_rows": ([3 * NEXP, NPAIR, P], BF16),
    "low_q": ([P, 1], F32), "low_k": ([P, 1], F32), "head_rows": ([P, GH], F32), "lower": ([P, EGRP * EGRP], F32),
    "gate_w": ([E, NEXP], F32), "gate_bias": ([P, NEXP], F32),
    "Wg": ([E, NEXP * INTER], F32), "Wu": ([E, NEXP * INTER], F32), "Wd": ([P, NPAIR, E], F32),
    "Sg": ([E, P], F32), "Su": ([E, P], F32), "Sd": ([P, E], F32),
}
for _a in ("a_", "b_"):
    SHAPES.update({_a + "WqR": ([E, NG, P], F32), _a + "WkR": ([E, NG, P], F32), _a + "bqR": ([P, NG], F32), _a + "bkR": ([P, NG], F32),
                   _a + "WvT": ([E, E], F32), _a + "WoT": ([E, E], F32), _a + "bv": ([P, E], F32), _a + "bo": ([1, E], F32)})
ROWS = ("gate_bias", "a_bv", "b_bv")


def build(nc, drams, x_dram, out):
    with ExitStack() as ctx:
        c = {n: ctx.enter_context(nc.sbuf_tensor(f"c_{n}", s, dt)) for n, (s, dt) in SHAPES.items()}
        x = ctx.enter_context(nc.sbuf_tensor("x_tokens", [P, NT, E], F32))
        pairs = []
        for n in SHAPES:
            dst = c[n][tuple(slice(None) for _ in SHAPES[n][0])]
            pairs.append((dst, drams[n].partition_broadcast(P) if n in ROWS else drams[n]))
        load_all(nc, pairs, x, x_dram)

        def ffn(name):
            with Mem(nc, name) as m:
                xnT = m.sb("xnT", [P, T])
                sc = m.sb("scores", [P, NT, NEXP])
                wT = m.sb("wT", [3 * NEXP, T], BF16)
                layernorm_transposed(nc, name + "_ln", c, x, xnT, sc)
                route(nc, name + "_route", c, sc, wT)
                experts(nc, name + "_exp", c, x, xnT, wT)

        def attention(name, body):
            with Mem(nc, name) as m:
                xnT = m.sb("xnT", [P, T])
                layernorm_transposed(nc, name + "_ln", c, x, xnT)
                body(nc, c, x, xnT)

        attention("att_a", banded_attention)
        ffn("ffn1")
        attention("att_b", head_softmax_attention)
        ffn("ffn2")
        store_x(nc, x, out)


def constants(bf16):
    k = {}
    k["ident"] = np.eye(P, dtype=np.float32)
    k["identb"] = np.eye(P, dtype=np.float32).astype(bf16)
    k["ones"] = np.ones((1, P), np.float32)
    band = np.zeros((QT, NQT, KW), np.float32)
    for t in range(NQT):
        q = t * QT + np.arange(QT)[:, None]
        key = t * QT - LEFT + np.arange(KW)[None, :]
        start = q // CHUNK * CHUNK
        ok = (key >= q - LEFT) & (key < start + CHUNK) & (key >= 0) & (key < S)
        ok |= (q >= S)
        band[:, t, :] = np.where(ok, 0.0, -BIG)
    k["band"] = band.astype(bf16)
    rows = np.zeros((3 * NEXP, NPAIR, P), np.float32)
    for part in range(3):
        for i in range(NPAIR):
            for e in range(2):
                rows[part * NEXP + 2 * i + e, i, e * INTER:(e + 1) * INTER] = 1.0
    k["pair_rows"] = rows.astype(bf16)
    part = np.arange(P) // D % 4
    k["low_q"] = np.where(part == 2, -1.0, 0.0).astype(np.float32)[:, None]
    k["low_k"] = np.where(part == 1, -1.0, 0.0).astype(np.float32)[:, None]
    k["head_rows"] = (np.arange(P)[:, None] // 32 == np.arange(GH)[None, :]).astype(np.float32)
    low = (np.arange(EGRP)[None, :] < np.arange(EGRP)[:, None]).astype(np.float32).reshape(1, -1)
    k["lower"] = np.repeat(low, P, axis=0)
    return k


def by_parts(w):
    w = w.reshape((NG, GH, 1, D) + w.shape[1:])
    out = np.zeros((NG, GH, 4, D) + w.shape[4:], w.dtype)
    out[:, :, 0:3] = w
    return out.reshape((NG, P) + w.shape[4:])


def kernel(**inputs):
    import ml_dtypes
    import concourse.bacc as _bacc
    from concourse.bass_utils import run_bass_kernel_spmd as _run

    a = {n: np.asarray(v) for n, v in inputs.items()}
    d = constants(ml_dtypes.bfloat16)
    for s, pre in (("a_", "L0_attn_a_"), ("b_", "L0_attn_b_")):
        for w in "qk":
            d[f"{s}W{w}R"] = by_parts(a[f"{pre}W{w}"]).transpose(2, 0, 1)
            d[f"{s}b{w}R"] = by_parts(a[f"{pre}b{w}"]).T
        d[s + "WvT"] = a[pre + "Wv"].T
        d[s + "WoT"] = a[pre + "Wo"].T
        d[s + "bv"] = a[pre + "bv"]
        d[s + "bo"] = a[pre + "bo"][None, :]
    f = "L0_ffn_"
    d["gate_w"] = a[f + "gate_w"].T
    d["gate_bias"] = a[f + "gate_bias"]
    d["Wg"] = a[f + "expert_gate"].transpose(2, 0, 1).reshape(E, NEXP * INTER)
    d["Wu"] = a[f + "expert_up"].transpose(2, 0, 1).reshape(E, NEXP * INTER)
    d["Wd"] = a[f + "expert_down"].transpose(0, 2, 1).reshape(NPAIR, P, E).transpose(1, 0, 2)
    d["Sg"] = a[f + "shared_gate"].T
    d["Su"] = a[f + "shared_up"].T
    d["Sd"] = a[f + "shared_down"].T
    x = np.ascontiguousarray(a["L0_attn_a_hidden_states"])

    nc = _bacc.Bacc("TRN2", target_bir_lowering=False, num_devices=1)
    arrays, drams = {}, {}
    for n in SHAPES:
        v = np.ascontiguousarray(d[n])
        arrays["in_" + n] = v
        drams[n] = nc.dram_tensor("in_" + n, v.shape, mybir.dt.from_np(v.dtype), kind="ExternalInput").ap()
    arrays["in_x"] = x
    x_dram = nc.dram_tensor("in_x", x.shape, F32, kind="ExternalInput").ap()
    out = nc.dram_tensor("out_x", x.shape, F32, kind="ExternalOutput").ap()
    build(nc, drams, x_dram, out)
    r = _run(nc, [arrays], core_ids=[0])
    return r.results[0]["out_x"]
```

```python
from contextlib import ExitStack

import numpy as np

import concourse.bass as bass
from concourse import mybir

F32 = mybir.dt.float32
F16 = mybir.dt.float16
BF16 = mybir.dt.bfloat16
ALU = mybir.AluOpType
ACT = mybir.ActivationFunctionType
AX = mybir.AxisListType

P = 128
B, S, E = 4, 1024, 128
T = B * S
NT = T // P
BT = S // P
NH, D = 16, 8
NG, GH = 4, 4
BLK = 512
NBLK = T // BLK
TB = BLK // P
SCALE = float(D) ** -0.5
EPS = 1e-5

CHUNK, LEFT = 10, 25
QT = 100
KW = QT + LEFT
NQT = -(-S // QT)
QPAD = NQT * QT
KPAD = QPAD + LEFT
HH = NH // 2
VA = D + 1

QS = 64
VSLOT = 32
NEXP, INTER = 32, 64
NPAIR = NEXP // 2
EGRP, EPG = 4, 8
TOPG = 2
ROUTED = 2.5
BIG = 1e30
ONE = 1


def tile_at(t, i):
    return t[:, bass.ds(i, 1), :].rearrange("p a e -> p (a e)")


class Chain:

    def __init__(self, eng, sem, base=0):
        self.eng, self.sem, self.base, self.n = eng, sem, base, 0

    def link(self, ins):
        self.n += 1
        ins.then_inc(self.sem, 1)
        self.eng.wait_ge(self.sem, ONE + self.base + self.n)


class Mem:

    def __init__(self, nc, stage):
        self.nc, self.stage, self.ctx, self.sems = nc, stage, ExitStack(), []

    def __enter__(self):
        return self

    def __exit__(self, *exc):
        return self.ctx.__exit__(*exc)

    def sb(self, name, shape, dt=F32):
        return self.ctx.enter_context(self.nc.sbuf_tensor(f"{self.stage}_{name}", shape, dt))

    def ps(self, name, shape, dt=F32):
        return self.ctx.enter_context(self.nc.psum_tensor(f"{self.stage}_{name}", shape, dt))

    def sem(self, name, by=None, credits=0):
        s = self.ctx.enter_context(self.nc.semaphore(f"{self.stage}_{name}"))
        if by:
            self.sems.append((s, by, credits))
        return s

    def start(self, eng, name):
        for s, by, credits in self.sems:
            if by == name:
                eng.sem_inc(s, ONE + credits)


def load_all(nc, pairs, x, x_dram):
    with Mem(nc, "load") as m:
        loaded = m.sem("loaded")
        block = m.ctx.enter_context(nc.Block())

        @block.sync
        def _(sp):
            sp.dma_start(x[:, :, :], x_dram.rearrange("b (t p) e -> p (b t) e", p=P)).then_inc(loaded, 16)
            for dst, src in pairs:
                sp.dma_start(dst, src).then_inc(loaded, 16)
            sp.wait_ge(loaded, 16 * (1 + len(pairs)))


def layernorm_transposed(nc, stage, c, x, xnT, scores=None):
    with Mem(nc, stage) as m:
        stats = m.sb("stats", [P, TB, 6])
        mv = m.sb("mv", [P, NT, 2])
        mvb = m.sb("mvb", [P, TB, 2])
        std = m.sb("std", [P, NT])
        rstd = m.sb("rstd", [P, NT])
        xn = m.sb("xn", [P, 2, TB, E])
        xs = m.sb("xs", [P, 2, BLK])
        turned = m.ps("turned", [P, 2, BLK])
        logits = m.ps("logits", [P, 2, BLK])
        chain, var_ready, std_ready = m.sem("chain", "dve"), m.sem("var_ready", "dve"), m.sem("std_ready", "act")
        xn_ready, turned_ready, xs_ready = m.sem("xn_ready", "dve"), m.sem("turned_ready", "pe", 1), m.sem("xs_ready", "act", 1)
        logits_ready, logits_read = m.sem("logits_ready", "pe"), m.sem("logits_read", "act", 1)
        dve_passed = m.sem("dve_passed")
        block = m.ctx.enter_context(nc.Block())

        @block.vector
        def _(dve):
            m.start(dve, "dve")
            with dve.Fori(0, NBLK) as k:
                ch = Chain(dve, chain, k * 3)
                for j in range(TB):
                    last = dve.bn_stats(stats[:, j, :], tile_at(x, k * TB + j))
                ch.link(last)
                dve.sem_inc(dve_passed, 1)
                for j in range(TB):
                    last = dve.bn_aggr(mvb[:, j, :], stats[:, j, :])
                ch.link(last)
                ch.link(dve.tensor_copy(mv[:, bass.ds(k * TB, TB), :], mvb[:, :, :]))
            dve.tensor_scalar(std[:, :], mv[:, :, 1], EPS, None, ALU.add).then_inc(var_ready, 1)
            dve.wait_ge(std_ready, ONE + 1)
            ch = Chain(dve, chain, 3 * NBLK)
            ch.link(dve.reciprocal(rstd[:, :], std[:, :]))
            with dve.Fori(0, NBLK // 2) as pair:
                k = pair * 2
                for u in range(2):
                    dve.wait_ge(turned_ready, ONE + k + u)
                    for j in range(TB):
                        t = k * TB + (u * TB + j)
                        last = dve.tensor_scalar(xn[:, u, j, :], tile_at(x, t), tile_at(mv, t)[:, 0:1], rstd[:, bass.ds(t, 1)], ALU.subtract, ALU.mult)
                    last.then_inc(xn_ready, 1)

        @block.tensor
        def _(pe):
            m.start(pe, "pe")
            with pe.Fori(0, NBLK // 2) as pair:
                k = pair * 2
                for u in range(2):
                    pe.wait_ge(xn_ready, ONE + k + u + 1)
                    pe.wait_ge(xs_ready, ONE + k + u)
                    for j in range(TB):
                        last = pe.transpose(turned[:, u, j * P:(j + 1) * P], xn[:, u, j, :], c["ident"][:, :])
                    last.then_inc(turned_ready, 1)
                    if scores is not None:
                        pe.wait_ge(xs_ready, ONE + k + u + 2)
                        pe.wait_ge(logits_read, ONE + k + u)
                        for j in range(TB):
                            last = pe.matmul(logits[:, u, j * NEXP:(j + 1) * NEXP], xs[:, u, j * P:(j + 1) * P],
                                             c["gate_w"][:, :], start=(j == 0), stop=True, skip_group_check=True)
                        last.then_inc(logits_ready, 1)

        @block.scalar
        def _(act):
            m.start(act, "act")
            act.wait_ge(var_ready, ONE + 1)
            act.activation(std[:, :], std[:, :], ACT.Sqrt).then_inc(std_ready, 1)
            if scores is not None:
                act.preload_act_table_set("sigmoid_and_others")
            with act.Fori(0, NBLK // 2) as pair:
                k = pair * 2
                for u in range(2):
                    act.wait_ge(turned_ready, ONE + k + u + 2)
                    if scores is not None:
                        act.activation(xs[:, u, :], turned[:, u, :], ACT.Copy)
                    act.activation(xnT[:, bass.ds(k * BLK + u * BLK, BLK)], turned[:, u, :], ACT.Copy).then_inc(xs_ready, 1)
                    if scores is not None:
                        act.wait_ge(logits_ready, ONE + k + u + 1)
                        act.activation(scores[:, bass.ds(k * TB + u * TB, TB), :],
                                       logits[:, u, 0:TB * NEXP].rearrange("p (t e) -> p t e", t=TB),
                                       ACT.Sigmoid).then_inc(logits_read, 1)


class Projections:

    UNITS = 2 * NG * (S // BLK)

    def __init__(self, m, c, att, qcols, kcols, koff, banks):
        self.c, self.att, self.koff, self.banks = c, att, koff, banks
        self.full = m.sb("full", [P, 2, BLK])
        self.high = m.sb("high", [P, 2, BLK], F16)
        self.parts = m.sb("parts", [P, 2, BLK], F16)
        self.QB = m.sb("QB", [P, NH, qcols], F16)
        self.KS = m.sb("KS", [P, NG, kcols], F16)
        self.xb = m.sb("xb", [P, kcols])
        self.xb_ready, self.proj_ready, self.full_ready = m.sem("xb_ready", "pool"), m.sem("proj_ready", "pe"), m.sem("full_ready", "act")
        self.passed = m.sem("passed")
        self.high_ready, self.parts_done, self.parts_chain = m.sem("high_ready", "pool"), m.sem("parts_done", "dve"), m.sem("parts_chain", "dve")

    def unit(self, u):
        kind, rest = divmod(u, self.UNITS // 2)
        g, h = divmod(rest, S // BLK)
        return kind, g, h

    def clear_pads(self, pool, sem):
        n = 0
        for t, lo, hi in ((self.xb, 0, self.koff), (self.xb, self.koff + S, self.xb.shape[1])):
            if hi > lo:
                pool.memset(t[:, lo:hi], 0.0).then_inc(sem, 1)
                n += 1
        for lo, hi in ((0, self.koff), (self.koff + S, self.KS.shape[2])):
            if hi > lo:
                pool.memset(self.KS[:, :, lo:hi], 0.0).then_inc(sem, 1)
                n += 1
        if self.QB.shape[2] > S:
            pool.memset(self.QB[:, :, S:], 0.0).then_inc(sem, 1)
            n += 1
        return n

    def on_pe(self, pe, b):
        pe.wait_ge(self.xb_ready, ONE + b + 1)
        for u in range(self.UNITS):
            kind, g, h = self.unit(u)
            w = self.c[self.att + ("WqR" if kind == 0 else "WkR")]
            if u >= 2:
                pe.wait_ge(self.full_ready, ONE + b * self.UNITS + u - 1)
            pe.matmul(self.banks[u % 2], w[:, g, :], self.xb[:, self.koff + h * BLK:self.koff + (h + 1) * BLK],
                      start=True, stop=True).then_inc(self.proj_ready, 1)

    def on_act(self, act, b):
        for u in range(self.UNITS):
            kind, g, h = self.unit(u)
            bias = self.c[self.att + ("bqR" if kind == 0 else "bkR")]
            act.wait_ge(self.proj_ready, ONE + b * self.UNITS + u + 1)
            if u >= 2:
                act.wait_ge(self.parts_done, ONE + b * self.UNITS + u - 1)
            act.activation(self.full[:, u % 2, :], self.banks[u % 2], ACT.Identity,
                           bias=bias[:, g:g + 1]).then_inc(self.full_ready, 1)

    def on_pool(self, pool, b):
        for u in range(self.UNITS):
            pool.wait_ge(self.full_ready, ONE + b * self.UNITS + u + 1)
            pool.sem_inc(self.passed, 1)
            pool.tensor_copy(self.high[:, u % 2, :], self.full[:, u % 2, :]).then_inc(self.high_ready, 1)

    def on_dve(self, dve, b):
        for u in range(self.UNITS):
            kind, g, h = self.unit(u)
            dve.wait_ge(self.high_ready, ONE + b * self.UNITS + u + 1)
            dve.wait_ge(self.parts_done, ONE + b * self.UNITS + u)
            if kind == 0:
                ch = Chain(dve, self.parts_chain, b * (self.UNITS // 2) + u)
                ch.link(dve.scalar_tensor_tensor(self.parts[:, u % 2, :], self.high[:, u % 2, :], self.c["low_q"][:, 0:1],
                                                 self.full[:, u % 2, :], ALU.mult, ALU.add))
                for n4 in range(GH):
                    last = dve.tensor_scalar(self.QB[:, GH * g + n4, h * BLK:(h + 1) * BLK], self.parts[:, u % 2, :],
                                             self.c["head_rows"][:, n4:n4 + 1], None, ALU.mult)
            else:
                last = dve.scalar_tensor_tensor(self.KS[:, g, self.koff + h * BLK:self.koff + (h + 1) * BLK],
                                                self.high[:, u % 2, :], self.c["low_k"][:, 0:1],
                                                self.full[:, u % 2, :], ALU.mult, ALU.add)
            last.then_inc(self.parts_done, 1)


def banded_attention(nc, c, x, xnT):
    NSTEP = 2 * NQT
    FRONT = NSTEP + 1
    with Mem(nc, "band") as m:
        score = m.ps("score", [P, 2, 2, BLK])
        turned = m.ps("turned", [P, 2, BLK])
        outp = m.ps("outp", [P, BLK])
        outT = m.ps("outT", [P, BLK])
        pr = Projections(m, c, "a_", QPAD + QT, KPAD + QT, LEFT, [score[:, 0, 0, :], score[:, 0, 1, :]])
        vw = m.sb("vw", [P, NQT * NH, VA])
        shift = m.sb("shift", [P, 2, HH], BF16)
        prob = m.sb("prob", [P, 2, HH, KW])
        probT = m.sb("probT", [P, 2, HH, QT])
        rden = m.sb("rden", [P, NH])
        on = m.sb("on", [P, NH, D])
        attT = m.sb("attT", [P, QPAD])
        cleared, v_ready, v_done = m.sem("cleared", "pool"), m.sem("v_ready", "pe"), m.sem("v_done", "dve")
        score_ready, shift_ready, shifted = m.sem("score_ready", "pe"), m.sem("shift_ready", "dve"), m.sem("shifted", "pe")
        prob_ready, turned_ready = m.sem("prob_ready", "act"), m.sem("turned_ready", "pe", 1)
        probT_ready, half_done = m.sem("probT_ready", "dve"), m.sem("half_done", "pe", 1)
        on_ready, onT_ready, attT_ready = m.sem("on_ready", "dve"), m.sem("onT_ready", "pe"), m.sem("attT_ready", "act")
        proj_ready, added, chain, passed = m.sem("proj_o_ready", "pe"), m.sem("added", "dve"), m.sem("chain", "dve"), m.sem("pe_passed")
        block = m.ctx.enter_context(nc.Block())
        NCLEAR = 6

        @block.gpsimd
        def _(pool):
            m.start(pool, "pool")
            n = pr.clear_pads(pool, cleared)
            pool.memset(vw[:, :, D:VA], 1.0).then_inc(cleared, 1)
            assert n + 1 == NCLEAR
            with pool.Fori(0, B) as b:
                pool.wait_ge(v_ready, ONE + b * NQT)
                pool.sem_inc(pr.passed, 1)
                pool.tensor_copy(pr.xb[:, LEFT:LEFT + S], xnT[:, bass.ds(b * S, S)]).then_inc(pr.xb_ready, 1)
                pr.on_pool(pool, b)

        @block.tensor
        def _(pe):
            m.start(pe, "pe")
            pe.wait_ge(cleared, ONE + NCLEAR)

            def scores_of(t, h):
                for j in range(HH):
                    n = HH * h + j
                    pe.matmul(score[0:QT, h, j // GH, (j % GH) * KW:(j % GH + 1) * KW],
                              pr.QB[:, n, bass.ds(t * QT, QT)], pr.KS[:, n // GH, bass.ds(t * QT, KW)],
                              start=(j % GH == 0), stop=False, skip_group_check=True)
                for k in range(2):
                    last = pe.matmul(score[0:QT, h, k, 0:GH * KW].rearrange("p (a w) -> p a w", a=GH), c["identb"][0:QT, 0:QT],
                                     tile_at(c["band"], t)[0:QT, :][:, None, :].broadcast_to([QT, GH, KW]),
                                     start=False, stop=False, skip_group_check=True)
                last.then_inc(score_ready, 1)

            def take_maximum(b, t, h):
                pe.wait_ge(shift_ready, ONE + b * FRONT + t * 2 + (h + 1))
                for k in range(2):
                    last = pe.matmul(score[0:QT, h, k, 0:GH * KW].rearrange("p (a w) -> p a w", a=GH), c["identb"][0:QT, 0:QT],
                                     shift[0:QT, h, k * GH:(k + 1) * GH][:, :, None].broadcast_to([QT, GH, KW]),
                                     start=False, stop=True, skip_group_check=True)
                last.then_inc(shifted, 1)

            def turn(step, h):
                pe.wait_ge(prob_ready, ONE + step + 1)
                pe.wait_ge(probT_ready, ONE + step)
                for j in range(HH):
                    last = pe.transpose(turned[0:KW, j // GH, (j % GH) * QT:(j % GH + 1) * QT],
                                        prob[0:QT, h, j, :], c["ident"][0:QT, 0:QT])
                last.then_inc(turned_ready, 1)

            def attend(step, tile, t, h):
                pe.wait_ge(probT_ready, ONE + step + 1)
                if h == 0:
                    pe.wait_ge(on_ready, ONE + tile)
                for j in range(HH):
                    n = HH * h + j
                    last = pe.matmul(outp[0:QT, n * VA:(n + 1) * VA], probT[0:KW, h, j, :], tile_at(vw, t * NH + n)[0:KW, :],
                                     start=(n == 0), stop=True, skip_group_check=True)
                last.then_inc(half_done, 1)

            def turn_output(tile):
                pe.wait_ge(on_ready, ONE + tile + 1)
                pe.wait_ge(attT_ready, ONE + tile)
                pe.transpose(outT[:, 0:QT], on[0:QT, :, :].rearrange("p n d -> p (n d)"),
                             c["ident"][0:QT, 0:QT]).then_inc(onT_ready, 1)

            def tile_of(b, t, first):
                step, tile = b * NSTEP + t * 2, b * NQT + t
                pe.wait_ge(prob_ready, ONE + step)
                scores_of(t, 1)
                take_maximum(b, t, 0)
                if not first:
                    turn(step - 1, 1)
                    attend(step - 2, tile - 1, t - 1, 0)
                pe.wait_ge(prob_ready, ONE + step + 1)
                scores_of(t + 1, 0)
                take_maximum(b, t, 1)
                turn(step, 0)
                if not first:
                    attend(step - 1, tile - 1, t - 1, 1)
                    turn_output(tile - 1)

            with pe.Fori(0, B) as b:
                pe.wait_ge(shift_ready, ONE + b * FRONT)
                pr.on_pe(pe, b)
                for w in range(NQT):
                    if w >= 2:
                        pe.wait_ge(v_done, ONE + b * NQT + w - 1)
                    pe.matmul(score[0:KW, 1, w % 2, 0:E], pr.xb[:, w * QT:w * QT + KW], c["a_WvT"][:, :],
                              start=True, stop=True).then_inc(v_ready, 1)
                pe.wait_ge(pr.parts_done, ONE + (b + 1) * pr.UNITS)
                pe.wait_ge(v_done, ONE + (b + 1) * NQT)
                scores_of(0, 0)
                tile_of(b, 0, True)
                with pe.Fori(1, NQT) as t:
                    tile_of(b, t, False)
                end, last_tile = (b + 1) * NSTEP, (b + 1) * NQT - 1
                turn(end - 1, 1)
                attend(end - 2, last_tile, NQT - 1, 0)
                attend(end - 1, last_tile, NQT - 1, 1)
                turn_output(last_tile)
                pe.wait_ge(attT_ready, ONE + (b + 1) * NQT)
                for j in range(BT):
                    if j >= 2:
                        pe.wait_ge(added, ONE + b * BT + j - 1)
                    o = (outp, outT)[j % 2]
                    pe.matmul(o[:, 0:E], attT[:, j * P:(j + 1) * P], c["a_WoT"][:, :], start=True, stop=False)
                    pe.matmul(o[:, 0:E], c["ones"][0:1, :], c["a_bo"][0:1, :], start=False, stop=True)\
                        .then_inc(proj_ready, 1)
                pe.wait_ge(added, ONE + (b + 1) * BT)

        @block.scalar
        def _(act):
            m.start(act, "act")

            def exponentials(step, h):
                act.wait_ge(shifted, ONE + step + 1)
                act.wait_ge(turned_ready, ONE + step)
                act.activation(prob[0:QT, h, :, :].rearrange("p (k a) w -> p k (a w)", k=2),
                               score[0:QT, h, :, 0:GH * KW], ACT.Exp, scale=SCALE).then_inc(prob_ready, 1)

            def copy_output(tile, t):
                act.wait_ge(onT_ready, ONE + tile + 1)
                act.activation(attT[:, bass.ds(t * QT, QT)], outT[:, 0:QT], ACT.Copy).then_inc(attT_ready, 1)

            with act.Fori(0, B) as b:
                pr.on_act(act, b)
                for h in range(2):
                    exponentials(b * NSTEP + h, h)
                act.wait_ge(proj_ready, ONE + b * BT)
                with act.Fori(1, NQT) as t:
                    for h in range(2):
                        exponentials(b * NSTEP + t * 2 + h, h)
                    copy_output(b * NQT + t - 1, t - 1)
                copy_output((b + 1) * NQT - 1, NQT - 1)

        @block.vector
        def _(dve):
            m.start(dve, "dve")

            def largest(b, front, h):
                dve.wait_ge(score_ready, ONE + front + 1)
                dve.wait_ge(shift_ready, ONE + front)
                dve.tensor_reduce(shift[0:QT, h, :].rearrange("p (k a) -> p k a", k=2),
                                  score[0:QT, h, :, 0:GH * KW].rearrange("p k (a w) -> p k a w", a=GH),
                                  AX.X, ALU.max, negate=True).then_inc(shift_ready, 1)

            def copy_turned(step, h):
                dve.wait_ge(turned_ready, ONE + step + 2)
                dve.wait_ge(half_done, ONE + step)
                dve.tensor_copy(probT[0:KW, h, :, :].rearrange("p (k a) q -> p k (a q)", k=2),
                                turned[0:KW, :, 0:GH * QT]).then_inc(probT_ready, 1)

            def divide(tile):
                dve.wait_ge(half_done, ONE + 2 * tile + 3)
                dve.wait_ge(on_ready, ONE + tile)
                o = outp[0:QT, 0:NH * VA].rearrange("p (n v) -> p n v", v=VA)
                ch = Chain(dve, chain, tile)
                ch.link(dve.reciprocal(rden[0:QT, :], o[:, :, D]))
                dve.wait_ge(onT_ready, ONE + tile)
                dve.tensor_tensor(on[0:QT, :, :], o[:, :, 0:D], rden[0:QT, :][:, :, None].broadcast_to([QT, NH, D]),
                                  ALU.mult).then_inc(on_ready, 1)

            def tile_of(b, t, first):
                step, tile, front = b * NSTEP + t * 2, b * NQT + t, b * FRONT + t * 2
                largest(b, front + 1, 1)
                if not first:
                    copy_turned(step - 1, 1)
                largest(b, front + 2, 0)
                copy_turned(step, 0)
                if not first:
                    divide(tile - 1)

            with dve.Fori(0, B) as b:
                dve.wait_ge(onT_ready, ONE + b * NQT)
                pr.on_dve(dve, b)
                for w in range(NQT):
                    dve.wait_ge(v_ready, ONE + b * NQT + w + 1)
                    dve.tensor_tensor(vw[0:KW, w * NH:(w + 1) * NH, 0:D], score[0:KW, 1, w % 2, 0:E].rearrange("p (n d) -> p n d", n=NH),
                                      c["a_bv"][0:KW, :].rearrange("p (n d) -> p n d", n=NH), ALU.add).then_inc(v_done, 1)
                largest(b, b * FRONT, 0)
                tile_of(b, 0, True)
                with dve.Fori(1, NQT) as t:
                    tile_of(b, t, False)
                copy_turned((b + 1) * NSTEP - 1, 1)
                divide((b + 1) * NQT - 1)
                for j in range(BT):
                    dve.wait_ge(proj_ready, ONE + b * BT + j + 1)
                    xt = tile_at(x, b * BT + j)
                    dve.tensor_tensor(xt, xt, (outp, outT)[j % 2][:, 0:E], ALU.add).then_inc(added, 1)


def head_softmax_attention(nc, c, x, xnT):
    NQ = S // P
    UB = NQ * BT
    FRONT = 2 * UB + 1
    LAG, RING = 2, 4
    with Mem(nc, "head") as m:
        score = m.ps("score", [P, 2, 2, BLK])
        recip = m.ps("recip", [P, 2, BLK])
        outp = m.ps("outp", [P, BLK])
        spare = m.ps("spare", [P, BLK])
        pr = Projections(m, c, "b_", S + P, S, 0, [score[:, 0, 0, :], score[:, 0, 1, :]])
        vs = m.sb("vs", [P, BT, (NH + 1) * VSLOT])
        shift = m.sb("shift", [P, 2, QS], BF16)
        ex = m.sb("ex", [P, RING, NH, P])
        half = m.sb("half", [P, NH // 2, P])
        den = m.sb("den", [P, 2, P])
        lnd = m.sb("lnd", [P, P])
        outT = m.sb("outT", [P, S])
        cleared, v_ready, v_done = m.sem("cleared", "pool"), m.sem("v_ready", "pe"), m.sem("v_done", "dve")
        score_ready, shift_ready, shifted = m.sem("score_ready", "pe"), m.sem("shift_ready", "dve"), m.sem("shifted", "pe")
        ex_ready, den_ready = m.sem("ex_ready", "act"), m.sem("den_ready", "pool")
        recip_ready, prob_ready = m.sem("recip_ready", "act", 1), m.sem("prob_ready", "dve", 1)
        av_done, outT_ready = m.sem("av_done", "pe", RING - 1), m.sem("outT_ready", "act")
        proj_ready, added = m.sem("proj_o_ready", "pe"), m.sem("added", "dve")
        vs_cleared = m.sem("vs_cleared", "dve")
        act_chain, pool_chain = m.sem("act_chain", "act"), m.sem("pool_chain", "pool")
        block = m.ctx.enter_context(nc.Block())
        NCLEAR = 1

        @block.gpsimd
        def _(pool):
            m.start(pool, "pool")
            n = pr.clear_pads(pool, cleared)
            assert n == NCLEAR
            with pool.Fori(0, B) as b:
                pool.wait_ge(v_ready, ONE + b * BT)
                pool.sem_inc(pr.passed, 1)
                pool.tensor_copy(pr.xb[:, :], xnT[:, bass.ds(b * S, S)]).then_inc(pr.xb_ready, 1)
                pr.on_pool(pool, b)
                with pool.Fori(0, NQ) as q:
                    for kt in range(BT):
                        unit = b * UB + q * BT + kt
                        e, hf = ex[:, kt % RING, :, :], half[:, :, :]
                        ch = Chain(pool, pool_chain, unit * 3)
                        pool.wait_ge(ex_ready, ONE + 2 * unit + 2)
                        pool.wait_ge(recip_ready, ONE + unit)
                        pool.wait_ge(den_ready, ONE + unit)
                        ch.link(pool.tensor_tensor(hf, e[:, 0:8, :], e[:, 8:16, :], ALU.add))
                        ch.link(pool.tensor_tensor(hf[:, 0:4, :], hf[:, 0:4, :], hf[:, 4:8, :], ALU.add))
                        ch.link(pool.tensor_tensor(hf[:, 0:2, :], hf[:, 0:2, :], hf[:, 2:4, :], ALU.add))
                        pool.tensor_tensor(den[:, kt % 2, :], hf[:, 0, :], hf[:, 1, :], ALU.add).then_inc(den_ready, 1)

        @block.tensor
        def _(pe):
            m.start(pe, "pe")
            pe.wait_ge(cleared, ONE + NCLEAR)

            def scores_of(q, s):
                kt, h = divmod(s % (2 * BT), 2)
                cols = q * P + (s // (2 * BT)) * P + h * QS
                for g in range(NG):
                    last = pe.matmul(score[:, s % 2, g // 2, (g % 2) * GH * QS:(g % 2 + 1) * GH * QS].rearrange("p (a w) -> p a w", a=GH),
                                     pr.KS[:, g, kt * P:(kt + 1) * P], pr.QB[:, g * GH:(g + 1) * GH, bass.ds(cols, QS)],
                                     start=(g % 2 == 0), stop=False, skip_group_check=True)
                last.then_inc(score_ready, 1)

            def attend(unit, chunk, kt):
                pe.wait_ge(prob_ready, ONE + unit + 2)
                if kt == 0:
                    pe.wait_ge(outT_ready, ONE + chunk)
                for n in range(NH):
                    g, n4 = divmod(n, GH)
                    at = n * VSLOT + VSLOT - D - n4 * D
                    last = pe.matmul(outp[g * 32:(g + 1) * 32, 0:P], vs[:, kt, at:at + 32], ex[:, kt % RING, n, :],
                                     start=(kt == 0 and n4 == 0), stop=(kt == BT - 1 and n4 == GH - 1), skip_group_check=True)
                last.then_inc(av_done, 1)

            def chunk_of(b, q, first):
                for s in range(2 * BT):
                    kt = s // 2
                    unit = b * UB + q * BT + kt
                    pe.wait_ge(ex_ready, ONE + 2 * unit + s % 2)
                    scores_of(q, s + 1)
                    pe.wait_ge(shift_ready, ONE + b * FRONT + q * (2 * BT) + (s + 1))
                    for k in range(2):
                        last = pe.matmul(score[:, s % 2, k, :].rearrange("p (a w) -> p a w", a=NH // 2), c["identb"][:, :],
                                         shift[:, s % 2, :][:, None, :].broadcast_to([P, NH // 2, QS]),
                                         start=False, stop=True, skip_group_check=True)
                    last.then_inc(shifted, 1)
                    if s % 2 == 1 and not (first and kt < LAG + 1):
                        back = (kt - LAG - 1) % BT
                        attend(unit - (LAG + 1), b * NQ + q - (1 if kt < LAG + 1 else 0), back)

            with pe.Fori(0, B) as b:
                pe.wait_ge(shift_ready, ONE + b * FRONT)
                pr.on_pe(pe, b)
                for w in range(BT):
                    if w >= 2:
                        pe.wait_ge(v_done, ONE + b * BT + w - 1)
                    pe.matmul(score[:, 1, w % 2, 0:E], pr.xb[:, w * P:(w + 1) * P], c["b_WvT"][:, :],
                              start=True, stop=True).then_inc(v_ready, 1)
                pe.wait_ge(pr.parts_done, ONE + (b + 1) * pr.UNITS)
                pe.wait_ge(v_done, ONE + (b + 1) * BT)
                scores_of(0, 0)
                chunk_of(b, 0, True)
                with pe.Fori(1, NQ) as q:
                    chunk_of(b, q, False)
                for kt in range(BT - LAG - 1, BT):
                    attend(b * UB + (UB - BT + kt), b * NQ + NQ - 1, kt)
                pe.wait_ge(outT_ready, ONE + (b + 1) * NQ)
                for j in range(BT):
                    if j >= 1:
                        pe.wait_ge(added, ONE + b * BT + j)
                    pe.matmul(spare[:, 0:E], outT[:, j * P:(j + 1) * P], c["b_WoT"][:, :], start=True, stop=False)
                    pe.matmul(spare[:, 0:E], c["ones"][0:1, :], c["b_bo"][0:1, :], start=False, stop=True)\
                        .then_inc(proj_ready, 1)
                pe.wait_ge(added, ONE + (b + 1) * BT)

        @block.scalar
        def _(act):
            m.start(act, "act")
            act.preload_act_table_set("natural_log_exp_and_others")

            def reciprocal_of(unit, kt):
                ch = Chain(act, act_chain, unit)
                act.wait_ge(den_ready, ONE + unit + 1)
                act.wait_ge(prob_ready, ONE + unit)
                ch.link(act.activation(lnd[:, :], den[:, kt % 2, :], ACT.Ln))
                act.activation(recip[:, kt % 2, 0:P], lnd[:, :], ACT.Exp, scale=-1.0).then_inc(recip_ready, 1)

            def copy_out(chunk, col):
                act.wait_ge(av_done, ONE + chunk * BT + BT + RING - 1)
                act.activation(outT[:, col], outp[:, 0:P], ACT.Copy).then_inc(outT_ready, 1)

            def chunk_of(b, q, first):
                for kt in range(BT):
                    unit = b * UB + q * BT + kt
                    for h in range(2):
                        act.wait_ge(shifted, ONE + 2 * unit + h + 1)
                        if h == 0:
                            act.wait_ge(av_done, ONE + unit)
                        act.activation(ex[:, kt % RING, :, h * QS:(h + 1) * QS],
                                       score[:, h, :, :].rearrange("p k (a w) -> p (k a) w", a=NH // 2),
                                       ACT.Exp, scale=SCALE).then_inc(ex_ready, 1)
                        if h == 0 and not (first and kt < LAG):
                            act.wait_ge(recip_ready, ONE + unit - LAG + 1)
                            reciprocal_of(unit - LAG, (kt - LAG) % BT)
                    if kt == LAG + 1 and not first:
                        copy_out(b * NQ + q - 1, bass.ds(q * P - P, P))

            with act.Fori(0, B) as b:
                pr.on_act(act, b)
                act.wait_ge(proj_ready, ONE + b * BT)
                chunk_of(b, 0, True)
                with act.Fori(1, NQ) as q:
                    chunk_of(b, q, False)
                for kt in range(BT - LAG, BT):
                    unit = b * UB + (UB - BT + kt)
                    act.wait_ge(recip_ready, ONE + unit + 1)
                    reciprocal_of(unit, kt)
                copy_out(b * NQ + NQ - 1, slice((NQ - 1) * P, NQ * P))

        @block.vector
        def _(dve):
            m.start(dve, "dve")
            dve.memset(vs[:, :, :], 0.0).then_inc(vs_cleared, 1)
            dve.wait_ge(vs_cleared, ONE + 1)

            def largest(front, s):
                dve.wait_ge(score_ready, ONE + front + 1)
                dve.wait_ge(shift_ready, ONE + front)
                dve.tensor_reduce(shift[:, s % 2, :], score[:, s % 2, :, :].rearrange("p k (a w) -> p w k a", a=NH // 2),
                                  AX.XY, ALU.max, negate=True).then_inc(shift_ready, 1)

            def weigh(unit, kt):
                dve.wait_ge(recip_ready, ONE + unit + 2)
                e = ex[:, kt % RING, :, :]
                dve.tensor_tensor(e, e, recip[:, kt % 2, 0:P][:, None, :].broadcast_to([P, NH, P]), ALU.mult).then_inc(prob_ready, 1)

            def chunk_of(b, q, first):
                for s in range(2 * BT):
                    kt = s // 2
                    largest(b * FRONT + q * (2 * BT) + (s + 1), s + 1)
                    if s % 2 == 1 and not (first and kt < LAG):
                        weigh(b * UB + q * BT + kt - LAG, (kt - LAG) % BT)

            with dve.Fori(0, B) as b:
                dve.wait_ge(av_done, ONE + b * UB + RING - 1)
                pr.on_dve(dve, b)
                for w in range(BT):
                    dve.wait_ge(v_ready, ONE + b * BT + w + 1)
                    dve.tensor_tensor(vs[:, w, 0:NH * VSLOT].rearrange("p (n s) -> p n s", n=NH)[:, :, VSLOT - D:],
                                      score[:, 1, w % 2, 0:E].rearrange("p (n d) -> p n d", n=NH),
                                      c["b_bv"][:, :].rearrange("p (n d) -> p n d", n=NH), ALU.add).then_inc(v_done, 1)
                largest(b * FRONT, 0)
                chunk_of(b, 0, True)
                with dve.Fori(1, NQ) as q:
                    chunk_of(b, q, False)
                for kt in range(BT - LAG, BT):
                    weigh(b * UB + (UB - BT + kt), kt)
                for j in range(BT):
                    dve.wait_ge(proj_ready, ONE + b * BT + j + 1)
                    xt = tile_at(x, b * BT + j)
                    dve.tensor_tensor(xt, xt, spare[:, 0:E], ALU.add).then_inc(added, 1)


def route(nc, stage, c, sc, wT):
    with Mem(nc, stage) as m:
        ch_ = m.sb("choice", [P, NT, NEXP])
        ta = m.sb("ta", [P, NT, NEXP])
        tb = m.sb("tb", [P, NT, NEXP])
        g1, g2, gs = m.sb("g1", [P, NT, EGRP]), m.sb("g2", [P, NT, EGRP]), m.sb("gs", [P, NT, EGRP])
        pa, pb = m.sb("pa", [P, NT, EGRP, EGRP]), m.sb("pb", [P, NT, EGRP, EGRP])
        top = m.sb("top", [P, NT, 8])
        tot = m.sb("tot", [P, NT])
        w3 = m.sb("w3", [P, NT, 3 * NEXP], BF16)
        pt = m.ps("pt", [P, 2, BLK])
        chain, w3_ready, pt_ready, pt_read = m.sem("chain", "dve"), m.sem("w3_ready", "dve"), m.sem("pt_ready", "pe"), m.sem("pt_read", "act")
        block = m.ctx.enter_context(nc.Block())

        @block.vector
        def _(dve):
            m.start(dve, "dve")
            L = Chain(dve, chain).link
            bg = c["gate_bias"][:, :][:, None, :].broadcast_to([P, NT, NEXP])
            by_group = lambda a: a[:, :, :].rearrange("p t (g e) -> p t g e", g=EGRP)
            L(dve.tensor_tensor(ch_[:, :, :], sc[:, :, :], bg, ALU.add))
            L(dve.tensor_reduce(g1[:, :, :], by_group(ch_), AX.X, ALU.max))
            for g in range(EGRP):
                last = dve.tensor_tensor(ta[:, :, g * EPG:(g + 1) * EPG], ch_[:, :, g * EPG:(g + 1) * EPG],
                                         g1[:, :, g:g + 1].broadcast_to([P, NT, EPG]), ALU.is_equal)
            L(last)
            L(dve.tensor_reduce(g2[:, :, :], by_group(ta), AX.X, ALU.add))
            L(dve.scalar_tensor_tensor(tb[:, :, :], ta[:, :, :], -BIG, ch_[:, :, :], ALU.mult, ALU.add))
            L(dve.tensor_scalar(g2[:, :, :], g2[:, :, :], 1.5, -BIG, ALU.is_lt, ALU.mult))
            L(dve.tensor_tensor(g2[:, :, :], g2[:, :, :], g1[:, :, :], ALU.add))
            L(dve.tensor_reduce(gs[:, :, :], by_group(tb), AX.X, ALU.max))
            L(dve.tensor_tensor(gs[:, :, :], gs[:, :, :], g2[:, :, :], ALU.max))
            L(dve.tensor_tensor(gs[:, :, :], gs[:, :, :], g1[:, :, :], ALU.add))
            for g in range(EGRP):
                own = gs[:, :, g:g + 1].broadcast_to([P, NT, EGRP])
                dve.tensor_tensor(pa[:, :, g, :], gs[:, :, :], own, ALU.is_ge)
                last = dve.tensor_tensor(pb[:, :, g, :], gs[:, :, :], own, ALU.is_gt)
            L(last)
            for g in range(EGRP):
                last = dve.tensor_tensor(pa[:, :, g, :], pa[:, :, g, :],
                                         c["lower"][:, g * EGRP:(g + 1) * EGRP][:, None, :].broadcast_to([P, NT, EGRP]), ALU.mult)
            L(last)
            L(dve.tensor_tensor(pa[:, :, :, :].rearrange("p t a b -> p (t a b)"), pa[:, :, :, :].rearrange("p t a b -> p (t a b)"),
                                pb[:, :, :, :].rearrange("p t a b -> p (t a b)"), ALU.max))
            L(dve.tensor_reduce(g1[:, :, :], pa[:, :, :, :], AX.X, ALU.add))
            L(dve.tensor_scalar(g1[:, :, :], g1[:, :, :], TOPG - 0.5, None, ALU.is_lt))
            for g in range(EGRP):
                last = dve.tensor_tensor(ta[:, :, g * EPG:(g + 1) * EPG], ch_[:, :, g * EPG:(g + 1) * EPG],
                                         g1[:, :, g:g + 1].broadcast_to([P, NT, EPG]), ALU.mult)
            L(last)
            L(dve.tensor_scalar(ta[:, :, :], ta[:, :, :], 0.0, None, ALU.add))
            for t in range(NT):
                last = dve.max(top[:, t, :], ta[:, t, :])
            L(last)
            for t in range(NT):
                last = dve.match_replace(tb[:, t, :], top[:, t, :], ta[:, t, :], -BIG)
            L(last)
            L(dve.tensor_scalar(tb[:, :, :], tb[:, :, :], -0.5 * BIG, None, ALU.is_lt))
            L(dve.tensor_tensor(ta[:, :, :], sc[:, :, :], tb[:, :, :], ALU.mult))
            L(dve.tensor_reduce(tot[:, :], ta[:, :, :], AX.X, ALU.add))
            L(dve.tensor_scalar(tot[:, :], tot[:, :], 1e-20, None, ALU.add))
            L(dve.reciprocal(tot[:, :], tot[:, :]))
            L(dve.tensor_tensor(ta[:, :, :], ta[:, :, :], tot[:, :][:, :, None].broadcast_to([P, NT, NEXP]), ALU.mult))
            L(dve.tensor_scalar(ta[:, :, :], ta[:, :, :], ROUTED, None, ALU.mult))
            L(dve.tensor_copy(w3[:, :, 0:NEXP], ta[:, :, :]))
            L(dve.tensor_tensor(tb[:, :, :], ta[:, :, :], w3[:, :, 0:NEXP], ALU.subtract))
            L(dve.tensor_copy(w3[:, :, NEXP:2 * NEXP], tb[:, :, :]))
            dve.tensor_tensor(w3[:, :, 2 * NEXP:3 * NEXP], tb[:, :, :], w3[:, :, NEXP:2 * NEXP], ALU.subtract).then_inc(w3_ready, 1)

        @block.tensor
        def _(pe):
            m.start(pe, "pe")
            pe.wait_ge(w3_ready, ONE + 1)
            with pe.Fori(0, NBLK // 2) as pair:
                k = pair * 2
                for u in range(2):
                    pe.wait_ge(pt_read, ONE + k + u)
                    for j in range(TB):
                        last = pe.matmul(pt[0:3 * NEXP, u, j * P:(j + 1) * P], tile_at(w3, k * TB + (u * TB + j)), c["identb"][:, :],
                                         start=(j == 0), stop=True, skip_group_check=True)
                    last.then_inc(pt_ready, 1)

        @block.scalar
        def _(act):
            m.start(act, "act")
            with act.Fori(0, NBLK // 2) as pair:
                k = pair * 2
                for u in range(2):
                    act.wait_ge(pt_ready, ONE + k + u + 1)
                    act.activation(wT[0:3 * NEXP, bass.ds(k * BLK + u * BLK, BLK)], pt[0:3 * NEXP, u, :], ACT.Copy).then_inc(pt_read, 1)


def experts(nc, stage, c, x, xnT, wT):
    NU = NPAIR + 1
    with Mem(nc, stage) as m:
        gate, up, wide = m.ps("gate", [P, 2, BLK]), m.ps("up", [P, 2, BLK]), m.ps("wide", [P, 2, BLK])
        down = m.ps("down", [P, BLK])
        back = m.ps("back", [P, BLK])
        sg, h1, h2 = m.sb("sg", [P, 2, BLK]), m.sb("h1", [P, BLK]), m.sb("h2", [P, 2, BLK])
        dT = m.sb("dT", [P, BLK])
        gate_ready, up_ready, sg_ready, h_ready = m.sem("gate_ready", "pe"), m.sem("up_ready", "pe"), m.sem("sg_ready", "act"), m.sem("h_ready", "dve", 1)
        dT_ready, back_ready, added, chain = m.sem("dT_ready", "act"), m.sem("back_ready", "pe"), m.sem("added", "dve"), m.sem("chain", "dve")
        down_done = m.sem("down_done", "pe", 1)
        block = m.ctx.enter_context(nc.Block())

        @block.tensor
        def _(pe):
            m.start(pe, "pe")
            with pe.Fori(0, NBLK) as k:
                xk = xnT[:, bass.ds(k * BLK, BLK)]

                def down_of(i):
                    pe.wait_ge(h_ready, ONE + k * NU + (i + 2))
                    if i == 0:
                        pe.wait_ge(dT_ready, ONE + k)
                    w = c["Wd"][:, i, :] if i < NPAIR else c["Sd"][:, :]
                    pe.matmul(down[:, :], w, h2[:, i % 2, :], start=(i == 0), stop=(i == NPAIR)).then_inc(down_done, 1)

                for i in range(NU):
                    pe.wait_ge(h_ready, ONE + k * NU + i + (i == 0))
                    gw = c["Wg"][:, i * P:(i + 1) * P] if i < NPAIR else c["Sg"][:, :]
                    uw = c["Wu"][:, i * P:(i + 1) * P] if i < NPAIR else c["Su"][:, :]
                    pe.matmul(gate[:, i % 2, :], gw, xk, start=True, stop=True).then_inc(gate_ready, 1)
                    last = pe.matmul(up[:, i % 2, :], uw, xk, start=True, stop=True)
                    if i < NPAIR:
                        last = pe.matmul(wide[:, i % 2, :], c["pair_rows"][0:3 * NEXP, i, :], wT[0:3 * NEXP, bass.ds(k * BLK, BLK)],
                                         start=True, stop=True)
                    last.then_inc(up_ready, 1)
                    if i >= 1:
                        down_of(i - 1)
                down_of(NPAIR)
                pe.wait_ge(dT_ready, ONE + k + 1)
                pe.wait_ge(added, ONE + k)
                for j in range(TB):
                    last = pe.transpose(back[:, j * P:(j + 1) * P], dT[:, j * P:(j + 1) * P], c["ident"][:, :])
                last.then_inc(back_ready, 1)

        @block.scalar
        def _(act):
            m.start(act, "act")
            act.preload_act_table_set("silu_and_others")
            with act.Fori(0, NBLK) as k:
                for i in range(NU):
                    act.wait_ge(gate_ready, ONE + k * NU + i + 1)
                    act.wait_ge(h_ready, ONE + k * NU + i + (i == 0))
                    act.activation(sg[:, i % 2, :], gate[:, i % 2, :], ACT.Silu).then_inc(sg_ready, 1)
                act.wait_ge(down_done, ONE + (k + 1) * NU + 1)
                act.wait_ge(back_ready, ONE + k)
                act.activation(dT[:, :], down[:, :], ACT.Copy).then_inc(dT_ready, 1)

        @block.vector
        def _(dve):
            m.start(dve, "dve")
            with dve.Fori(0, NBLK) as k:
                for i in range(NU):
                    ch = Chain(dve, chain, k * (NU - 1) + i)
                    dve.wait_ge(sg_ready, ONE + k * NU + i + 1)
                    dve.wait_ge(up_ready, ONE + k * NU + i + 1)
                    dve.wait_ge(down_done, ONE + k * NU + i + (i == 0))
                    if i < NPAIR:
                        dve.wait_ge(h_ready, ONE + k * NU + i + 1)
                        ch.link(dve.tensor_tensor(h1[:, :], sg[:, i % 2, :], up[:, i % 2, :], ALU.mult))
                        dve.tensor_tensor(h2[:, i % 2, :], h1[:, :], wide[:, i % 2, :], ALU.mult).then_inc(h_ready, 1)
                    else:
                        dve.tensor_tensor(h2[:, i % 2, :], sg[:, i % 2, :], up[:, i % 2, :], ALU.mult).then_inc(h_ready, 1)
                dve.wait_ge(back_ready, ONE + k + 1)
                xt = x[:, bass.ds(k * TB, TB), :]
                dve.tensor_tensor(xt, xt, back[:, :].rearrange("p (t e) -> p t e", t=TB), ALU.add).then_inc(added, 1)


def store_x(nc, x, out):
    with Mem(nc, "store") as m:
        stored = m.sem("stored")
        block = m.ctx.enter_context(nc.Block())

        @block.sync
        def _(sp):
            sp.dma_start(out.rearrange("b (t p) e -> p (b t) e", p=P), x[:, :, :]).then_inc(stored, 16)
            sp.wait_ge(stored, 16)


SHAPES = {
    "ident": ([P, P], F32), "identb": ([P, P], BF16), "ones": ([1, P], F32),
    "band": ([QT, NQT + 1, KW], BF16), "pair_rows": ([3 * NEXP, NPAIR, P], BF16),
    "low_q": ([P, 1], F32), "low_k": ([P, 1], F32), "head_rows": ([P, GH], F32), "lower": ([P, EGRP * EGRP], F32),
    "gate_w": ([E, NEXP], F32), "gate_bias": ([P, NEXP], F32),
    "Wg": ([E, NEXP * INTER], F32), "Wu": ([E, NEXP * INTER], F32), "Wd": ([P, NPAIR, E], F32),
    "Sg": ([E, P], F32), "Su": ([E, P], F32), "Sd": ([P, E], F32),
}
for _a in ("a_", "b_"):
    SHAPES.update({_a + "WqR": ([E, NG, P], F32), _a + "WkR": ([E, NG, P], F32), _a + "bqR": ([P, NG], F32), _a + "bkR": ([P, NG], F32),
                   _a + "WvT": ([E, E], F32), _a + "WoT": ([E, E], F32), _a + "bv": ([P, E], F32), _a + "bo": ([1, E], F32)})
ROWS = ("gate_bias", "a_bv", "b_bv")


def build(nc, drams, x_dram, out):
    with ExitStack() as ctx:
        c = {n: ctx.enter_context(nc.sbuf_tensor(f"c_{n}", s, dt)) for n, (s, dt) in SHAPES.items()}
        x = ctx.enter_context(nc.sbuf_tensor("x_tokens", [P, NT, E], F32))
        pairs = []
        for n in SHAPES:
            dst = c[n][tuple(slice(None) for _ in SHAPES[n][0])]
            pairs.append((dst, drams[n].partition_broadcast(P) if n in ROWS else drams[n]))
        load_all(nc, pairs, x, x_dram)

        def ffn(name):
            with Mem(nc, name) as m:
                xnT = m.sb("xnT", [P, T])
                sc = m.sb("scores", [P, NT, NEXP])
                wT = m.sb("wT", [3 * NEXP, T], BF16)
                layernorm_transposed(nc, name + "_ln", c, x, xnT, sc)
                route(nc, name + "_route", c, sc, wT)
                experts(nc, name + "_exp", c, x, xnT, wT)

        def attention(name, body):
            with Mem(nc, name) as m:
                xnT = m.sb("xnT", [P, T])
                layernorm_transposed(nc, name + "_ln", c, x, xnT)
                body(nc, c, x, xnT)

        attention("att_a", banded_attention)
        ffn("ffn1")
        attention("att_b", head_softmax_attention)
        ffn("ffn2")
        store_x(nc, x, out)


def constants(bf16):
    k = {}
    k["ident"] = np.eye(P, dtype=np.float32)
    k["identb"] = np.eye(P, dtype=np.float32).astype(bf16)
    k["ones"] = np.ones((1, P), np.float32)
    band = np.zeros((QT, NQT + 1, KW), np.float32)
    for t in range(NQT):
        q = t * QT + np.arange(QT)[:, None]
        key = t * QT - LEFT + np.arange(KW)[None, :]
        start = q // CHUNK * CHUNK
        ok = (key >= q - LEFT) & (key < start + CHUNK) & (key >= 0) & (key < S)
        ok |= (q >= S)
        band[:, t, :] = np.where(ok, 0.0, -BIG)
    k["band"] = band.astype(bf16)
    rows = np.zeros((3 * NEXP, NPAIR, P), np.float32)
    for part in range(3):
        for i in range(NPAIR):
            for e in range(2):
                rows[part * NEXP + 2 * i + e, i, e * INTER:(e + 1) * INTER] = 1.0
    k["pair_rows"] = rows.astype(bf16)
    part = np.arange(P) // D % 4
    k["low_q"] = np.where(part == 2, -1.0, 0.0).astype(np.float32)[:, None]
    k["low_k"] = np.where(part == 1, -1.0, 0.0).astype(np.float32)[:, None]
    k["head_rows"] = (np.arange(P)[:, None] // 32 == np.arange(GH)[None, :]).astype(np.float32)
    low = (np.arange(EGRP)[None, :] < np.arange(EGRP)[:, None]).astype(np.float32).reshape(1, -1)
    k["lower"] = np.repeat(low, P, axis=0)
    return k


def by_parts(w):
    w = w.reshape((NG, GH, 1, D) + w.shape[1:])
    out = np.zeros((NG, GH, 4, D) + w.shape[4:], w.dtype)
    out[:, :, 0:3] = w
    return out.reshape((NG, P) + w.shape[4:])


def kernel(**inputs):
    import ml_dtypes
    import concourse.bacc as _bacc
    from concourse.bass_utils import run_bass_kernel_spmd as _run

    a = {n: np.asarray(v) for n, v in inputs.items()}
    d = constants(ml_dtypes.bfloat16)
    for s, pre in (("a_", "L0_attn_a_"), ("b_", "L0_attn_b_")):
        for w in "qk":
            d[f"{s}W{w}R"] = by_parts(a[f"{pre}W{w}"]).transpose(2, 0, 1)
            d[f"{s}b{w}R"] = by_parts(a[f"{pre}b{w}"]).T
        d[s + "WvT"] = a[pre + "Wv"].T
        d[s + "WoT"] = a[pre + "Wo"].T
        d[s + "bv"] = a[pre + "bv"]
        d[s + "bo"] = a[pre + "bo"][None, :]
    f = "L0_ffn_"
    d["gate_w"] = a[f + "gate_w"].T
    d["gate_bias"] = a[f + "gate_bias"]
    d["Wg"] = a[f + "expert_gate"].transpose(2, 0, 1).reshape(E, NEXP * INTER)
    d["Wu"] = a[f + "expert_up"].transpose(2, 0, 1).reshape(E, NEXP * INTER)
    d["Wd"] = a[f + "expert_down"].transpose(0, 2, 1).reshape(NPAIR, P, E).transpose(1, 0, 2)
    d["Sg"] = a[f + "shared_gate"].T
    d["Su"] = a[f + "shared_up"].T
    d["Sd"] = a[f + "shared_down"].T
    x = np.ascontiguousarray(a["L0_attn_a_hidden_states"])

    nc = _bacc.Bacc("TRN2", target_bir_lowering=False, num_devices=1)
    arrays, drams = {}, {}
    for n in SHAPES:
        v = np.ascontiguousarray(d[n])
        arrays["in_" + n] = v
        drams[n] = nc.dram_tensor("in_" + n, v.shape, mybir.dt.from_np(v.dtype), kind="ExternalInput").ap()
    arrays["in_x"] = x
    x_dram = nc.dram_tensor("in_x", x.shape, F32, kind="ExternalInput").ap()
    out = nc.dram_tensor("out_x", x.shape, F32, kind="ExternalOutput").ap()
    build(nc, drams, x_dram, out)
    r = _run(nc, [arrays], core_ids=[0])
    return r.results[0]["out_x"]
```

```python
from contextlib import ExitStack

import numpy as np

import concourse.bass as bass
from concourse import mybir

F32 = mybir.dt.float32
F16 = mybir.dt.float16
BF16 = mybir.dt.bfloat16
ALU = mybir.AluOpType
ACT = mybir.ActivationFunctionType
AX = mybir.AxisListType

P = 128
B, S, E = 4, 1024, 128
T = B * S
NT = T // P
BT = S // P
NH, D = 16, 8
NG, GH = 4, 4
BLK = 512
NBLK = T // BLK
TB = BLK // P
SCALE = float(D) ** -0.5
EPS = 1e-5

CHUNK, LEFT = 10, 25
QT = 100
KW = QT + LEFT
NQT = -(-S // QT)
QPAD = NQT * QT
KPAD = QPAD + LEFT
HH = NH // 2
VA = D + 1

QS = 64
VSLOT = 32
NEXP, INTER = 32, 64
NPAIR = NEXP // 2
EGRP, EPG = 4, 8
TOPG = 2
ROUTED = 2.5
BIG = 1e30
WSCALE = 16.0
ASCALE = 4.0
NU = NPAIR + 1
ONE = 1


def tile_at(t, i):
    return t[:, bass.ds(i, 1), :].rearrange("p a e -> p (a e)")


class Chain:

    def __init__(self, eng, sem, base=0):
        self.eng, self.sem, self.base, self.n = eng, sem, base, 0

    def link(self, ins):
        self.n += 1
        ins.then_inc(self.sem, 1)
        self.eng.wait_ge(self.sem, ONE + self.base + self.n)


class Mem:

    def __init__(self, nc, stage):
        self.nc, self.stage, self.ctx, self.sems = nc, stage, ExitStack(), []

    def __enter__(self):
        return self

    def __exit__(self, *exc):
        return self.ctx.__exit__(*exc)

    def sb(self, name, shape, dt=F32):
        return self.ctx.enter_context(self.nc.sbuf_tensor(f"{self.stage}_{name}", shape, dt))

    def ps(self, name, shape, dt=F32):
        return self.ctx.enter_context(self.nc.psum_tensor(f"{self.stage}_{name}", shape, dt))

    def sem(self, name, by=None, credits=0):
        s = self.ctx.enter_context(self.nc.semaphore(f"{self.stage}_{name}"))
        if by:
            self.sems.append((s, by, credits))
        return s

    def start(self, eng, name):
        for s, by, credits in self.sems:
            if by == name:
                eng.sem_inc(s, ONE + credits)


def product(pe, out, w, i, hi, lo, start=True, stop=True):
    pe.matmul(out, w[:, i, 0, :], hi, start=start, stop=False)
    pe.matmul(out, w[:, i, 0, :], lo, start=False, stop=False)
    return pe.matmul(out, w[:, i, 1, :], hi, start=False, stop=stop)


class Weights:

    def __init__(self, m, weights, bias_drams):
        nb = len(bias_drams)
        self.weights = weights
        self.whole = m.sb("whole", [P, len(weights), NU, P])
        self.bias, self.bias_full = m.sb("bias", [2, nb, 2 * NG, P]), m.sb("bias_full", [2, nb, 2 * NG, P])
        self.bias_high = m.sb("bias_high", [2, nb, 2 * NG, P], F16)
        self.loaded, self.pairs_loaded = m.sem("weights_loaded"), m.sem("loaded")
        self.loads = [(self.whole[:, n, u:u + src.shape[1], :], src) for n, (_, _, srcs) in enumerate(weights) for u, src in srcs]
        self.loads += [(self.bias[:, n, :, :], src.partition_broadcast(2)) for n, src in enumerate(bias_drams)]


def load_all(nc, m, w, pairs, x, x_dram):
    x_loaded, first_loaded = m.sem("x_loaded"), m.sem("first_loaded")
    with nc.Block() as block:

        @block.sync
        def _(sp):
            sp.dma_start(x[:, 0:NT // 2, :], x_dram[0:B // 2].rearrange("b (t p) e -> p (b t) e", p=P)).then_inc(x_loaded, 16)
            for dst, src in w.loads:
                sp.dma_start(dst, src).then_inc(w.loaded, 16)
            sp.wait_ge(x_loaded, 2 * 16)
            sp.wait_ge(first_loaded, 16)

        @block.scalar
        def _(act):
            act.dma_start(x[:, NT // 2:, :], x_dram[B // 2:].rearrange("b (t p) e -> p (b t) e", p=P)).then_inc(x_loaded, 16)
            act.dma_start(*pairs[0]).then_inc(first_loaded, 16)
            for dst, src in pairs[1:]:
                act.dma_start(dst, src).then_inc(w.pairs_loaded, 16)


def split_weights(nc, m, c, w, pairs):
    high_ready, low_ready = m.sem("high_ready"), m.sem("low_ready")
    with nc.Block() as block:

        @block.scalar
        def _(act):
            act.wait_ge(w.loaded, 16 * len(w.loads))
            for t in (w.bias_full, w.bias_high):
                last = act.activation(t[:, :, :, :], w.bias[:, :, :, :], ACT.Copy, scale=ASCALE)
            last.then_inc(high_ready, 1)
            for n, (parts, scale, _) in enumerate(w.weights):
                act.activation(parts[:, :, 0, :], w.whole[:, n, 0:parts.shape[1], :], ACT.Copy, scale=scale).then_inc(high_ready, 1)

        @block.vector
        def _(dve):
            dve.wait_ge(w.loaded, 16 * len(w.loads))
            dve.wait_ge(w.pairs_loaded, 16 * (len(pairs) - 1))
            dve.wait_ge(high_ready, 1)
            dve.scalar_tensor_tensor(c["bias_parts"][:, :, :, :], w.bias_high[:, :, :, :], c["bias_rows"][:, 0:1], w.bias_full[:, :, :, :],
                                     ALU.mult, ALU.add).then_inc(low_ready, 1)
            for n, (parts, scale, _) in enumerate(w.weights):
                dve.wait_ge(high_ready, n + 2)
                dve.scalar_tensor_tensor(parts[:, :, 1, :], w.whole[:, n, 0:parts.shape[1], :], scale, parts[:, :, 0, :],
                                         ALU.mult, ALU.subtract).then_inc(low_ready, 1)


def layernorm_transposed(nc, stage, c, x, xnT, pad=0, scores=None):
    with Mem(nc, stage) as m:
        stats = m.sb("stats", [P, NT, 6])
        mv = m.sb("mv", [P, NT, 2])
        std = m.sb("std", [P, NT])
        rstd = m.sb("rstd", [P, NT])
        xn = m.sb("xn", [P, 2, TB, E])
        xs = m.sb("xs", [P, 2, BLK])
        turned = m.ps("turned", [P, 2, BLK])
        logits = m.ps("logits", [P, 2, BLK])
        chain, var_ready, std_ready = m.sem("chain", "dve"), m.sem("var_ready", "dve"), m.sem("std_ready", "act")
        xn_ready, turned_ready, xs_ready = m.sem("xn_ready", "dve"), m.sem("turned_ready", "pe", 1), m.sem("xs_ready", "act", 1)
        high_ready, low_ready = m.sem("high_ready", "act"), m.sem("low_ready", "dve", 1)
        logits_ready, logits_read = m.sem("logits_ready", "pe"), m.sem("logits_read", "act", 1)
        block = m.ctx.enter_context(nc.Block())

        @block.vector
        def _(dve):
            m.start(dve, "dve")
            L = Chain(dve, chain).link
            for t in range(NT):
                last = dve.bn_stats(stats[:, t, :], x[:, t, :])
            L(last)
            for t in range(NT):
                last = dve.bn_aggr(mv[:, t, :], stats[:, t, :])
            L(last)
            dve.tensor_scalar(std[:, :], mv[:, :, 1], EPS, None, ALU.add).then_inc(var_ready, 1)
            dve.wait_ge(std_ready, ONE + 1)
            L(dve.reciprocal(rstd[:, :], std[:, :]))

            def normalise(k, u):
                dve.wait_ge(turned_ready, ONE + k)
                for j in range(TB):
                    t = k * TB + j
                    last = dve.tensor_scalar(xn[:, u, j, :], tile_at(x, t), tile_at(mv, t)[:, 0:1], rstd[:, bass.ds(t, 1)], ALU.subtract, ALU.mult)
                last.then_inc(xn_ready, 1)

            def low_part(k, u):
                dve.wait_ge(high_ready, ONE + k + 1)
                at = bass.ds(k * BLK + pad, BLK)
                dve.tensor_tensor(xnT[:, 1, at], turned[:, u, :], xnT[:, 0, at],
                                  ALU.subtract).then_inc(low_ready, 1)

            def pair_of(k, last):
                for u in range(2):
                    if not (last and u == 1):
                        normalise(k + (u + 1), (u + 1) % 2)
                    low_part(k + u, u)

            normalise(0, 0)
            with dve.Fori(0, NBLK // 2 - 1) as pair:
                pair_of(pair * 2, False)
            pair_of(NBLK - 2, True)

        @block.tensor
        def _(pe):
            m.start(pe, "pe")

            def logits_of(k, u):
                pe.wait_ge(xs_ready, ONE + k + 2)
                pe.wait_ge(logits_read, ONE + k)
                for j in range(TB):
                    last = pe.matmul(logits[:, u, j * NEXP:(j + 1) * NEXP], xs[:, u, j * P:(j + 1) * P],
                                     c["gate_w"][:, :], start=(j == 0), stop=True, skip_group_check=True)
                last.then_inc(logits_ready, 1)

            def pair_of(k, first):
                for u in range(2):
                    pe.wait_ge(xn_ready, ONE + k + u + 1)
                    pe.wait_ge(low_ready, ONE + k + u)
                    for j in range(TB):
                        last = pe.transpose(turned[:, u, j * P:(j + 1) * P], xn[:, u, j, :], c["ident"][:, :])
                    last.then_inc(turned_ready, 1)
                    if scores is not None and not (first and u == 0):
                        logits_of(k + (u - 1), 1 - u)

            pair_of(0, True)
            with pe.Fori(1, NBLK // 2) as pair:
                pair_of(pair * 2, False)
            if scores is not None:
                logits_of(NBLK - 1, 1)

        @block.scalar
        def _(act):
            m.start(act, "act")
            act.wait_ge(var_ready, ONE + 1)
            act.activation(std[:, :], std[:, :], ACT.Sqrt).then_inc(std_ready, 1)
            if scores is not None:
                act.preload_act_table_set("sigmoid_and_others")

            def score_of(k, u):
                act.wait_ge(logits_ready, ONE + k + 1)
                act.activation(scores[:, bass.ds(k * TB, TB), :], logits[:, u, 0:TB * NEXP].rearrange("p (t e) -> p t e", t=TB),
                               ACT.Sigmoid).then_inc(logits_read, 1)

            def pair_of(k, first):
                for u in range(2):
                    act.wait_ge(turned_ready, ONE + k + u + 2)
                    if scores is not None:
                        act.activation(xs[:, u, :], turned[:, u, :], ACT.Copy).then_inc(xs_ready, 1)
                    act.activation(xnT[:, 0, bass.ds(k * BLK + (u * BLK + pad), BLK)], turned[:, u, :], ACT.Copy).then_inc(high_ready, 1)
                    if scores is not None and not (first and u == 0):
                        score_of(k + (u - 1), 1 - u)

            pair_of(0, True)
            with act.Fori(1, NBLK // 2) as pair:
                pair_of(pair * 2, False)
            if scores is not None:
                score_of(NBLK - 1, 1)


class Projections:

    UNITS = 2 * NG * (S // BLK)
    QUNITS = UNITS // 2
    RING = 4
    ON_ACT = 2

    def __init__(self, m, c, att, xnT, by_head, pads, hcols, gcols, banks):
        self.c, self.att, self.xnT, self.banks = c, att, xnT, banks
        self.pad, self.hpad, self.gpad = pads
        self.by_head = "qk".index(by_head)
        self.low_rows = [c["low_q"], c["low_k"]]
        self.high = m.sb("high", [P, self.RING, BLK], F16)
        self.parts = m.sb("parts", [P, 2, BLK], F16)
        self.HB = m.sb("HB", [P, NH, hcols], F16)
        self.GR = m.sb("GR", [P, NG, gcols], F16)
        self.proj_ready, self.high_ready = m.sem("proj_ready", "pe"), m.sem("high_ready", "act")
        self.parts_done, self.parts_ready, self.heads_done = m.sem("parts_done", "dve"), m.sem("parts_ready", "dve"), m.sem("heads_done", "act", 2)

    def unit(self, u):
        g, h = divmod(u // 2, S // BLK)
        return u % 2, g, h

    def clear_pads(self, pool, sem):
        n = 0
        for t, lo, hi in ((self.xnT, 0, self.pad), (self.xnT, self.pad + T, self.xnT.shape[2]), (self.HB, 0, self.hpad),
                          (self.HB, self.hpad + S, self.HB.shape[2]), (self.GR, 0, self.gpad), (self.GR, self.gpad + S, self.GR.shape[2])):
            if hi > lo:
                pool.memset(t[:, :, lo:hi], 0.0).then_inc(sem, 1)
                n += 1
        return n

    def on_pe(self, pe, b):
        for u in range(self.UNITS):
            kind, g, h = self.unit(u)
            at = bass.ds(b * S + (self.pad + h * BLK), BLK)
            bank = self.banks[u % self.RING]
            if u >= self.RING:
                pe.wait_ge(self.parts_done, ONE + b * self.UNITS + u - self.RING + 1)
            weight = (kind ^ self.by_head) * NG + g
            product(pe, bank, self.c[self.att + "parts"], weight, self.xnT[:, 0, at], self.xnT[:, 1, at], stop=False)
            pe.matmul(bank, self.c["bias_parts"][:, "ab".index(self.att[0]), weight, :], self.c["ones2"][:, :],
                      start=False, stop=True).then_inc(self.proj_ready, 1)

    def values_on_pe(self, pe, b, starts, rows, ready):
        w = self.c[self.att + "parts"]
        for i, start in enumerate(starts):
            bank, j = self.banks[i // TB], i % TB
            if j == 0:
                pe.wait_ge(self.parts_done, ONE + (b + 1) * self.UNITS - self.RING + i // TB + 1)
            at = bass.ds(b * S + start, rows)
            out = bank[0:rows, j * P:(j + 1) * P]
            pe.matmul(out, self.xnT[:, 0, at], w[:, 2 * NG, 0, :], start=(j == 0), stop=False, skip_group_check=True)
            pe.matmul(out, self.xnT[:, 0, at], w[:, 2 * NG, 1, :], start=False, stop=False, skip_group_check=True)
            last = pe.matmul(out, self.xnT[:, 1, at], w[:, 2 * NG, 0, :], start=False, stop=True, skip_group_check=True)
            if j == TB - 1 or i == len(starts) - 1:
                last.then_inc(ready, 1)

    def on_act(self, act, b):
        for u in range(self.UNITS):
            act.wait_ge(self.proj_ready, ONE + b * self.UNITS + u + 1)
            if u >= self.RING:
                act.wait_ge(self.parts_done, ONE + b * self.UNITS + u - self.RING + 1)
            act.activation(self.high[:, u % self.RING, :], self.banks[u % self.RING], ACT.Copy).then_inc(self.high_ready, 1)
            if u >= 3 and u % 2 == 1:
                self.place_heads(act, b, u - 3)
        self.place_heads(act, b, self.UNITS - 2)

    def place_heads(self, act, b, u):
        _, g, h = self.unit(u)
        act.wait_ge(self.parts_ready, ONE + b * self.QUNITS + u // 2 + 1)
        for n4 in range(self.ON_ACT):
            last = act.activation(self.HB[:, GH * g + n4, self.hpad + h * BLK:self.hpad + (h + 1) * BLK], self.parts[:, u // 2 % 2, :],
                                  ACT.Copy, scale=self.c["head_rows"][:, n4:n4 + 1])
        last.then_inc(self.heads_done, 1)

    def on_dve(self, dve, b):
        for u in range(self.UNITS):
            kind, g, h = self.unit(u)
            high, whole = self.high[:, u % self.RING, :], self.banks[u % self.RING]
            dve.wait_ge(self.high_ready, ONE + b * self.UNITS + u + 1)
            if kind == 0:
                dve.wait_ge(self.parts_done, ONE + b * self.UNITS + u)
                dve.wait_ge(self.heads_done, ONE + b * self.QUNITS + u // 2)
                buf = u // 2 % 2
                ch = Chain(dve, self.parts_ready, b * self.QUNITS + u // 2)
                ch.link(dve.scalar_tensor_tensor(self.parts[:, buf, :], high, self.low_rows[self.by_head][:, 0:1], whole, ALU.mult, ALU.add))
                for n4 in range(self.ON_ACT, GH):
                    last = dve.tensor_scalar(self.HB[:, GH * g + n4, self.hpad + h * BLK:self.hpad + (h + 1) * BLK], self.parts[:, buf, :],
                                             self.c["head_rows"][:, n4:n4 + 1], None, ALU.mult)
            else:
                last = dve.scalar_tensor_tensor(self.GR[:, g, self.gpad + h * BLK:self.gpad + (h + 1) * BLK],
                                                high, self.low_rows[1 - self.by_head][:, 0:1], whole, ALU.mult, ALU.add)
            last.then_inc(self.parts_done, 1)


def project_out(pe, c, att, out, attT, n):
    for j in range(TB):
        o = out[:, j * P:(j + 1) * P]
        pe.matmul(o, attT[:, (n * TB + j) * P:(n * TB + j + 1) * P], c[att + "WoT"][:, :], start=(j == 0), stop=False, skip_group_check=True)
        last = pe.matmul(o, c["ones"][0:1, :], c[att + "bo"][0:1, :], start=False, stop=True, skip_group_check=True)
    return last


def banded_attention(nc, c, x, xnT):
    NSTEP = 2 * NQT
    FRONT = NSTEP + 1
    NVG = -(-NQT // TB)
    WAIT_PROB = 2
    with Mem(nc, "band") as m:
        score = m.ps("score", [P, 2, 2, BLK])
        turned = m.ps("turned", [P, 2, BLK])
        outp = m.ps("outp", [P, BLK])
        outT = m.ps("outT", [P, BLK])
        pr = Projections(m, c, "a_", xnT, "k", (LEFT, LEFT, 0), KPAD + QT, QPAD + QT, [score[:, u // 2, u % 2, :] for u in range(4)])
        vw = m.sb("vw", [P, NQT * NH, VA])
        shift = m.sb("shift", [P, 2, HH], BF16)
        prob = m.sb("prob", [P, 2, HH, KW])
        probT = m.sb("probT", [P, 2, HH, QT])
        rden = m.sb("rden", [P, NH])
        on = m.sb("on", [P, NH, D])
        attT = m.sb("attT", [P, QPAD])
        warm = m.sb("warm", [P, 2 * P], BF16)
        cleared, v_ready, v_done = m.sem("cleared", "pool"), m.sem("v_ready", "pe"), m.sem("v_done", "dve")
        score_ready, shift_ready, shifted = m.sem("score_ready", "pe"), m.sem("shift_ready", "dve"), m.sem("shifted", "pe")
        prob_ready, turned_ready = m.sem("prob_ready", "act"), m.sem("turned_ready", "pe", 1)
        probT_ready, half_done = m.sem("probT_ready", "dve"), m.sem("half_done", "pe", 1)
        on_ready, onT_ready, attT_ready = m.sem("on_ready", "dve"), m.sem("onT_ready", "pe"), m.sem("attT_ready", "act")
        proj_ready, added, chain = m.sem("proj_o_ready", "pe"), m.sem("added", "dve"), m.sem("chain", "dve")
        block = m.ctx.enter_context(nc.Block())
        NCLEAR = 7

        @block.gpsimd
        def _(pool):
            m.start(pool, "pool")
            n = pr.clear_pads(pool, cleared)
            pool.memset(vw[:, :, D:VA], 1.0).then_inc(cleared, 1)
            pool.memset(warm[:, :], 0.0).then_inc(cleared, 1)
            assert n + 2 == NCLEAR

        @block.tensor
        def _(pe):
            m.start(pe, "pe")
            pe.wait_ge(cleared, ONE + NCLEAR)

            def scores_of(t, h):
                for k in range(2):
                    g = 2 * h + k
                    pe.matmul(score[0:QT, h, k, 0:GH * KW].rearrange("p (a w) -> p a w", a=GH), pr.GR[:, g, bass.ds(t * QT, QT)],
                              pr.HB[:, g * GH:(g + 1) * GH, bass.ds(t * QT, KW)], start=True, stop=False, skip_group_check=True)
                for k in range(2):
                    last = pe.matmul(score[0:QT, h, k, 0:GH * KW].rearrange("p (a w) -> p a w", a=GH), c["identb"][0:QT, 0:QT],
                                     tile_at(c["band"], t)[0:QT, :][:, None, :].broadcast_to([QT, GH, KW]),
                                     start=False, stop=False, skip_group_check=True)
                last.then_inc(score_ready, 1)

            def keep_clock(n):
                for _ in range(n):
                    pe.matmul(turned[:, 0, 0:2 * P], c["identb"][:, :], warm[:, :], start=True, stop=True, skip_group_check=True)

            def take_maximum(b, t, h):
                pe.wait_ge(shift_ready, ONE + b * FRONT + t * 2 + (h + 1))
                for k in range(2):
                    last = pe.matmul(score[0:QT, h, k, 0:GH * KW].rearrange("p (a w) -> p a w", a=GH), c["identb"][0:QT, 0:QT],
                                     shift[0:QT, h, k * GH:(k + 1) * GH][:, :, None].broadcast_to([QT, GH, KW]),
                                     start=False, stop=True, skip_group_check=True)
                last.then_inc(shifted, 1)

            def turn(step, h):
                pe.wait_ge(probT_ready, ONE + step)
                keep_clock(WAIT_PROB)
                pe.wait_ge(prob_ready, ONE + step + 1)
                for j in range(HH):
                    last = pe.transpose(turned[0:KW, j // GH, (j % GH) * QT:(j % GH + 1) * QT],
                                        prob[0:QT, h, j, :], c["ident"][0:QT, 0:QT])
                last.then_inc(turned_ready, 1)

            def attend(step, tile, t, h):
                pe.wait_ge(probT_ready, ONE + step + 1)
                if h == 0:
                    pe.wait_ge(on_ready, ONE + tile)
                for j in range(HH):
                    n = HH * h + j
                    last = pe.matmul(outp[0:QT, n * VA:(n + 1) * VA], probT[0:KW, h, j, :], tile_at(vw, t * NH + n)[0:KW, :],
                                     start=(n == 0), stop=True, skip_group_check=True)
                last.then_inc(half_done, 1)

            def turn_output(tile):
                pe.wait_ge(on_ready, ONE + tile + 1)
                pe.wait_ge(attT_ready, ONE + tile)
                pe.transpose(outT[:, 0:QT], on[0:QT, :, :].rearrange("p n d -> p (n d)"),
                             c["ident"][0:QT, 0:QT]).then_inc(onT_ready, 1)

            def tile_of(b, t, before):
                step, tile = b * NSTEP + t * 2, b * NQT + t
                pe.wait_ge(prob_ready, ONE + step)
                scores_of(t, 1)
                take_maximum(b, t, 0)
                if before:
                    turn(step - 1, 1)
                    attend(step - 2, tile - 1, t - 1, 0)
                if before == 2:
                    turn_output(tile - 2)
                pe.wait_ge(prob_ready, ONE + step + 1)
                scores_of(t + 1, 0)
                take_maximum(b, t, 1)
                turn(step, 0)
                if before:
                    attend(step - 1, tile - 1, t - 1, 1)

            with pe.Fori(0, B) as b:
                pe.wait_ge(shift_ready, ONE + b * FRONT)
                pr.on_pe(pe, b)
                pr.values_on_pe(pe, b, [w * QT for w in range(NQT)], KW, v_ready)
                pe.wait_ge(pr.parts_done, ONE + (b + 1) * pr.UNITS)
                pe.wait_ge(pr.heads_done, ONE + (b + 1) * pr.QUNITS + 2)
                pe.wait_ge(v_done, ONE + (b + 1) * NVG)
                pe.wait_ge(added, ONE + b * 2)
                scores_of(0, 0)
                tile_of(b, 0, 0)
                tile_of(b, 1, 1)
                with pe.Fori(2, NQT) as t:
                    tile_of(b, t, 2)
                end, last_tile = (b + 1) * NSTEP, (b + 1) * NQT - 1
                turn(end - 1, 1)
                attend(end - 2, last_tile, NQT - 1, 0)
                turn_output(last_tile - 1)
                attend(end - 1, last_tile, NQT - 1, 1)
                turn_output(last_tile)
                pe.wait_ge(attT_ready, ONE + (b + 1) * NQT)
                for n, o in enumerate((outp, outT)):
                    project_out(pe, c, "a_", o, attT, n).then_inc(proj_ready, 1)

        @block.scalar
        def _(act):
            m.start(act, "act")

            def exponentials(step, h):
                act.wait_ge(shifted, ONE + step + 1)
                act.wait_ge(turned_ready, ONE + step)
                act.activation(prob[0:QT, h, :, :].rearrange("p (k a) w -> p k (a w)", k=2),
                               score[0:QT, h, :, 0:GH * KW], ACT.Exp, scale=SCALE / ASCALE ** 2).then_inc(prob_ready, 1)

            def copy_output(tile, t):
                act.wait_ge(onT_ready, ONE + tile + 1)
                act.activation(attT[:, bass.ds(t * QT, QT)], outT[:, 0:QT], ACT.Copy).then_inc(attT_ready, 1)

            with act.Fori(0, B) as b:
                pr.on_act(act, b)
                for h in range(2):
                    exponentials(b * NSTEP + h, h)
                act.wait_ge(proj_ready, ONE + b * 2)
                for h in range(2):
                    exponentials(b * NSTEP + 2 + h, h)
                with act.Fori(2, NQT) as t:
                    exponentials(b * NSTEP + t * 2, 0)
                    copy_output(b * NQT + t - 2, t - 2)
                    exponentials(b * NSTEP + t * 2 + 1, 1)
                for t in (NQT - 2, NQT - 1):
                    copy_output(b * NQT + t, t)

        @block.vector
        def _(dve):
            m.start(dve, "dve")

            def largest(b, front, h):
                dve.wait_ge(score_ready, ONE + front + 1)
                dve.wait_ge(shift_ready, ONE + front)
                dve.tensor_reduce(shift[0:QT, h, :].rearrange("p (k a) -> p k a", k=2),
                                  score[0:QT, h, :, 0:GH * KW].rearrange("p k (a w) -> p k a w", a=GH),
                                  AX.X, ALU.max, negate=True).then_inc(shift_ready, 1)

            def copy_turned(step, h):
                dve.wait_ge(turned_ready, ONE + step + 2)
                dve.wait_ge(half_done, ONE + step)
                dve.tensor_copy(probT[0:KW, h, :, :].rearrange("p (k a) q -> p k (a q)", k=2),
                                turned[0:KW, :, 0:GH * QT]).then_inc(probT_ready, 1)

            def divide(tile):
                dve.wait_ge(half_done, ONE + 2 * tile + 3)
                dve.wait_ge(on_ready, ONE + tile)
                o = outp[0:QT, 0:NH * VA].rearrange("p (n v) -> p n v", v=VA)
                ch = Chain(dve, chain, tile)
                ch.link(dve.reciprocal(rden[0:QT, :], o[:, :, D]))
                dve.wait_ge(onT_ready, ONE + tile)
                dve.tensor_tensor(on[0:QT, :, :], o[:, :, 0:D], rden[0:QT, :][:, :, None].broadcast_to([QT, NH, D]),
                                  ALU.mult).then_inc(on_ready, 1)

            def tile_of(b, t, first):
                step, tile, front = b * NSTEP + t * 2, b * NQT + t, b * FRONT + t * 2
                largest(b, front + 1, 1)
                if not first:
                    copy_turned(step - 1, 1)
                largest(b, front + 2, 0)
                copy_turned(step, 0)
                if not first:
                    divide(tile - 1)

            with dve.Fori(0, B) as b:
                dve.wait_ge(onT_ready, ONE + b * NQT)
                pr.on_dve(dve, b)
                for g in range(NVG):
                    n = min(TB, NQT - g * TB)
                    dve.wait_ge(v_ready, ONE + b * NVG + g + 1)
                    for j in range(n):
                        w = g * TB + j
                        last = dve.scalar_tensor_tensor(
                            vw[0:KW, w * NH:(w + 1) * NH, 0:D], pr.banks[g][0:KW, j * E:(j + 1) * E].rearrange("p (n d) -> p n d", n=NH),
                            1 / ASCALE, c["a_bv"][0:KW, :].rearrange("p (n d) -> p n d", n=NH), ALU.mult, ALU.add)
                    last.then_inc(v_done, 1)
                largest(b, b * FRONT, 0)
                tile_of(b, 0, True)
                with dve.Fori(1, NQT) as t:
                    tile_of(b, t, False)
                copy_turned((b + 1) * NSTEP - 1, 1)
                divide((b + 1) * NQT - 1)
                for n, o in enumerate((outp, outT)):
                    dve.wait_ge(proj_ready, ONE + b * 2 + n + 1)
                    xt = x[:, bass.ds(b * BT + n * TB, TB), :]
                    dve.tensor_tensor(xt, xt, o[:, :].rearrange("p (t e) -> p t e", t=TB), ALU.add).then_inc(added, 1)


def head_softmax_attention(nc, c, x, xnT):
    NQ = S // P
    UB = NQ * BT
    FRONT = 2 * UB + 1
    NVG = BT // TB
    LAG, RING = 2, 4
    ON_DVE = 13
    with Mem(nc, "head") as m:
        score = m.ps("score", [P, 2, 2, BLK])
        den = m.ps("den", [P, 2, BLK])
        outp = m.ps("outp", [P, BLK])
        spare = m.ps("spare", [P, BLK])
        pr = Projections(m, c, "b_", xnT, "q", (0, 0, 0), S + P, S, [score[:, u // 2, u % 2, :] for u in range(4)])
        vs = m.sb("vs", [P, BT, (NH + 1) * VSLOT])
        shift = m.sb("shift", [P, 2, QS], BF16)
        ex = m.sb("ex", [P, RING, NH, P])
        half = m.sb("half", [P, 2, NH // 2, P])
        recip = m.sb("recip", [P, 2, P])
        lnd = m.sb("lnd", [P, P])
        outT = m.sb("outT", [P, S])
        cleared, v_ready, v_done = m.sem("cleared", "pool"), m.sem("v_ready", "pe"), m.sem("v_done", "dve")
        score_ready, shift_ready, shifted = m.sem("score_ready", "pe"), m.sem("shift_ready", "dve"), m.sem("shifted", "pe")
        ex_ready, den_ready = m.sem("ex_ready", "act"), m.sem("den_ready", "pe", 1)
        quarter_ready, rest_ready = m.sem("quarter_ready", "pool"), m.sem("rest_ready", "pool", 1)
        recip_ready, prob_ready = m.sem("recip_ready", "act", 1), m.sem("prob_ready", "dve", 1)
        av_done, outT_ready = m.sem("av_done", "pe", RING - 1), m.sem("outT_ready", "act")
        proj_ready, added = m.sem("proj_o_ready", "pe"), m.sem("added", "dve")
        vs_cleared = m.sem("vs_cleared", "dve")
        act_chain, pool_chain = m.sem("act_chain", "act"), m.sem("pool_chain", "pool")
        block = m.ctx.enter_context(nc.Block())
        NCLEAR = 1

        @block.gpsimd
        def _(pool):
            m.start(pool, "pool")
            n = pr.clear_pads(pool, cleared)
            assert n == NCLEAR

            def sum_heads(unit, kt):
                e, hf = ex[:, kt % RING, :, :], half[:, kt % 2, :, :]
                ch = Chain(pool, pool_chain, unit)
                pool.wait_ge(ex_ready, ONE + 2 * unit + 2)
                pool.wait_ge(den_ready, ONE + unit)
                ch.link(pool.tensor_tensor(hf, e[:, 0:8, :], e[:, 8:16, :], ALU.add))
                pool.tensor_tensor(hf[:, 0:4, :], hf[:, 0:4, :], hf[:, 4:8, :], ALU.add).then_inc(quarter_ready, 1)

            def weigh_rest(unit, kt):
                pool.wait_ge(recip_ready, ONE + unit + 2)
                e = ex[:, kt % RING, ON_DVE:, :]
                pool.tensor_tensor(e, e, recip[:, kt % 2, :][:, None, :].broadcast_to([P, NH - ON_DVE, P]),
                                   ALU.mult).then_inc(rest_ready, 1)

            def chunk_of(b, q, first):
                for kt in range(BT):
                    unit = b * UB + q * BT + kt
                    if not (first and kt < LAG):
                        weigh_rest(unit - LAG, (kt - LAG) % BT)
                    sum_heads(unit, kt)

            with pool.Fori(0, B) as b:
                chunk_of(b, 0, True)
                with pool.Fori(1, NQ) as q:
                    chunk_of(b, q, False)
                for kt in range(BT - LAG, BT):
                    weigh_rest(b * UB + (UB - BT + kt), kt)

        @block.tensor
        def _(pe):
            m.start(pe, "pe")
            pe.wait_ge(cleared, ONE + NCLEAR)

            def scores_of(q, s):
                kt, h = divmod(s % (2 * BT), 2)
                cols = q * P + (s // (2 * BT)) * P + h * QS
                for g in range(NG):
                    last = pe.matmul(score[:, s % 2, g // 2, (g % 2) * GH * QS:(g % 2 + 1) * GH * QS].rearrange("p (a w) -> p a w", a=GH),
                                     pr.GR[:, g, kt * P:(kt + 1) * P], pr.HB[:, g * GH:(g + 1) * GH, bass.ds(cols, QS)],
                                     start=(g % 2 == 0), stop=False, skip_group_check=True)
                last.then_inc(score_ready, 1)

            def attend(unit, chunk, kt, half_of_heads):
                if half_of_heads == 0:
                    pe.wait_ge(prob_ready, ONE + unit + 2)
                    if kt == 0:
                        pe.wait_ge(outT_ready, ONE + chunk)
                else:
                    pe.wait_ge(rest_ready, ONE + unit + 2)
                for n in range(half_of_heads * HH, (half_of_heads + 1) * HH):
                    g, n4 = divmod(n, GH)
                    at = n * VSLOT + VSLOT - D - n4 * D
                    last = pe.matmul(outp[g * 32:(g + 1) * 32, 0:P], vs[:, kt, at:at + 32], ex[:, kt % RING, n, :],
                                     start=(kt == 0 and n4 == 0), stop=(kt == BT - 1 and n4 == GH - 1), skip_group_check=True)
                if half_of_heads == 1:
                    last.then_inc(av_done, 1)

            def take_maximum(b, q, s):
                pe.wait_ge(shift_ready, ONE + b * FRONT + q * (2 * BT) + (s + 1))
                for k in range(2):
                    last = pe.matmul(score[:, s % 2, k, :].rearrange("p (a w) -> p a w", a=NH // 2), c["identb"][:, :],
                                     shift[:, s % 2, :][:, None, :].broadcast_to([P, NH // 2, QS]),
                                     start=False, stop=True, skip_group_check=True)
                last.then_inc(shifted, 1)

            def denominator_of(unit, kt):
                pe.wait_ge(quarter_ready, ONE + unit + 1)
                pe.wait_ge(recip_ready, ONE + unit)
                for k in range(4):
                    last = pe.matmul(den[:, kt % 2, 0:P], c["ident"][:, :], half[:, kt % 2, k, :], start=(k == 0), stop=(k == 3))
                last.then_inc(den_ready, 1)

            def chunk_of(b, q, first):
                for s in range(2 * BT):
                    kt = s // 2
                    unit = b * UB + q * BT + kt
                    if s % 2 == 0:
                        take_maximum(b, q, s)
                    pe.wait_ge(ex_ready, ONE + 2 * unit + s % 2)
                    scores_of(q, s + 1)
                    if s % 2 != 0:
                        take_maximum(b, q, s)
                    if not (first and kt < LAG + 1):
                        back = (kt - LAG - 1) % BT
                        attend(unit - (LAG + 1), b * NQ + q - (1 if kt < LAG + 1 else 0), back, s % 2)
                    if s % 2 == 1 and not (first and kt == 0):
                        denominator_of(unit - 1, (kt - 1) % BT)

            with pe.Fori(0, B) as b:
                pe.wait_ge(shift_ready, ONE + b * FRONT)
                pr.on_pe(pe, b)
                pr.values_on_pe(pe, b, [w * P for w in range(BT)], P, v_ready)
                pe.wait_ge(pr.parts_done, ONE + (b + 1) * pr.UNITS)
                pe.wait_ge(pr.heads_done, ONE + (b + 1) * pr.QUNITS + 2)
                pe.wait_ge(v_done, ONE + (b + 1) * NVG)
                pe.wait_ge(added, ONE + b * 2)
                scores_of(0, 0)
                chunk_of(b, 0, True)
                with pe.Fori(1, NQ) as q:
                    chunk_of(b, q, False)
                denominator_of(b * UB + (UB - 1), BT - 1)
                for kt in range(BT - LAG - 1, BT):
                    for half_of_heads in range(2):
                        attend(b * UB + (UB - BT + kt), b * NQ + NQ - 1, kt, half_of_heads)
                pe.wait_ge(outT_ready, ONE + (b + 1) * NQ)
                for n, o in enumerate((outp, spare)):
                    project_out(pe, c, "b_", o, outT, n).then_inc(proj_ready, 1)

        @block.scalar
        def _(act):
            m.start(act, "act")
            act.preload_act_table_set("natural_log_exp_and_others")

            def reciprocal_of(unit, kt):
                ch = Chain(act, act_chain, unit)
                act.wait_ge(den_ready, ONE + unit + 2)
                act.wait_ge(prob_ready, ONE + unit)
                act.wait_ge(rest_ready, ONE + unit)
                ch.link(act.activation(lnd[:, :], den[:, kt % 2, 0:P], ACT.Ln))
                act.activation(recip[:, kt % 2, :], lnd[:, :], ACT.Exp, scale=-1.0).then_inc(recip_ready, 1)

            def copy_out(chunk, col):
                act.wait_ge(av_done, ONE + chunk * BT + BT + RING - 1)
                act.activation(outT[:, col], outp[:, 0:P], ACT.Copy).then_inc(outT_ready, 1)

            def chunk_of(b, q, first):
                for kt in range(BT):
                    unit = b * UB + q * BT + kt
                    for h in range(2):
                        act.wait_ge(shifted, ONE + 2 * unit + h + 1)
                        if h == 0:
                            act.wait_ge(av_done, ONE + unit)
                        act.activation(ex[:, kt % RING, :, h * QS:(h + 1) * QS],
                                       score[:, h, :, :].rearrange("p k (a w) -> p (k a) w", a=NH // 2),
                                       ACT.Exp, scale=SCALE / ASCALE ** 2).then_inc(ex_ready, 1)
                        if h == 0 and kt == LAG + 1 and not first:
                            copy_out(b * NQ + q - 1, bass.ds(q * P - P, P))
                        if h == 0 and not (first and kt < LAG):
                            act.wait_ge(recip_ready, ONE + unit - LAG + 1)
                            reciprocal_of(unit - LAG, (kt - LAG) % BT)

            with act.Fori(0, B) as b:
                pr.on_act(act, b)
                act.wait_ge(proj_ready, ONE + b * 2)
                chunk_of(b, 0, True)
                with act.Fori(1, NQ) as q:
                    chunk_of(b, q, False)
                for kt in range(BT - LAG, BT):
                    unit = b * UB + (UB - BT + kt)
                    act.wait_ge(recip_ready, ONE + unit + 1)
                    reciprocal_of(unit, kt)
                copy_out(b * NQ + NQ - 1, slice((NQ - 1) * P, NQ * P))

        @block.vector
        def _(dve):
            m.start(dve, "dve")
            dve.memset(vs[:, :, :], 0.0).then_inc(vs_cleared, 1)
            dve.wait_ge(vs_cleared, ONE + 1)

            def largest(front, s):
                dve.wait_ge(score_ready, ONE + front + 1)
                dve.wait_ge(shift_ready, ONE + front)
                dve.tensor_reduce(shift[:, s % 2, :], score[:, s % 2, :, :].rearrange("p k (a w) -> p w k a", a=NH // 2),
                                  AX.XY, ALU.max, negate=True).then_inc(shift_ready, 1)

            def weigh(unit, kt):
                dve.wait_ge(recip_ready, ONE + unit + 2)
                e = ex[:, kt % RING, 0:ON_DVE, :]
                dve.tensor_tensor(e, e, recip[:, kt % 2, :][:, None, :].broadcast_to([P, ON_DVE, P]), ALU.mult).then_inc(prob_ready, 1)

            def chunk_of(b, q, first):
                for s in range(2 * BT):
                    kt = s // 2
                    largest(b * FRONT + q * (2 * BT) + (s + 1), s + 1)
                    if s % 2 == 1 and not (first and kt < LAG):
                        weigh(b * UB + q * BT + kt - LAG, (kt - LAG) % BT)

            with dve.Fori(0, B) as b:
                dve.wait_ge(av_done, ONE + b * UB + RING - 1)
                pr.on_dve(dve, b)
                for g in range(NVG):
                    dve.wait_ge(v_ready, ONE + b * NVG + g + 1)
                    for j in range(TB):
                        last = dve.scalar_tensor_tensor(
                            vs[:, g * TB + j, 0:NH * VSLOT].rearrange("p (n s) -> p n s", n=NH)[:, :, VSLOT - D:],
                            pr.banks[g][:, j * E:(j + 1) * E].rearrange("p (n d) -> p n d", n=NH), 1 / ASCALE,
                            c["b_bv"][:, :].rearrange("p (n d) -> p n d", n=NH), ALU.mult, ALU.add)
                    last.then_inc(v_done, 1)
                largest(b * FRONT, 0)
                chunk_of(b, 0, True)
                with dve.Fori(1, NQ) as q:
                    chunk_of(b, q, False)
                for kt in range(BT - LAG, BT):
                    weigh(b * UB + (UB - BT + kt), kt)
                for n, o in enumerate((outp, spare)):
                    dve.wait_ge(proj_ready, ONE + b * 2 + n + 1)
                    xt = x[:, bass.ds(b * BT + n * TB, TB), :]
                    dve.tensor_tensor(xt, xt, o[:, :].rearrange("p (t e) -> p t e", t=TB), ALU.add).then_inc(added, 1)


def route(nc, stage, c, sc, wT):
    with Mem(nc, stage) as m:
        ch_ = m.sb("choice", [P, NT, NEXP])
        ta = m.sb("ta", [P, NT, NEXP])
        tb = m.sb("tb", [P, NT, NEXP])
        g1, g2, gs = m.sb("g1", [P, NT, EGRP]), m.sb("g2", [P, NT, EGRP]), m.sb("gs", [P, NT, EGRP])
        pa, pb = m.sb("pa", [P, NT, EGRP, EGRP]), m.sb("pb", [P, NT, EGRP, EGRP])
        top = m.sb("top", [P, NT, 8])
        tot = m.sb("tot", [P, NT])
        w3 = m.sb("w3", [P, NT, 3 * NEXP], BF16)
        pt = m.ps("pt", [P, 2, BLK])
        chain, w3_ready, pt_ready, pt_read = m.sem("chain", "dve"), m.sem("w3_ready", "dve"), m.sem("pt_ready", "pe"), m.sem("pt_read", "act", 1)
        block = m.ctx.enter_context(nc.Block())

        @block.vector
        def _(dve):
            m.start(dve, "dve")
            L = Chain(dve, chain).link
            bg = c["gate_bias"][:, :][:, None, :].broadcast_to([P, NT, NEXP])
            by_group = lambda a: a[:, :, :].rearrange("p t (g e) -> p t g e", g=EGRP)
            L(dve.tensor_tensor(ch_[:, :, :], sc[:, :, :], bg, ALU.add))
            L(dve.tensor_reduce(g1[:, :, :], by_group(ch_), AX.X, ALU.max))
            for g in range(EGRP):
                last = dve.tensor_tensor(ta[:, :, g * EPG:(g + 1) * EPG], ch_[:, :, g * EPG:(g + 1) * EPG],
                                         g1[:, :, g:g + 1].broadcast_to([P, NT, EPG]), ALU.is_equal)
            L(last)
            L(dve.tensor_reduce(g2[:, :, :], by_group(ta), AX.X, ALU.add))
            L(dve.scalar_tensor_tensor(tb[:, :, :], ta[:, :, :], -BIG, ch_[:, :, :], ALU.mult, ALU.add))
            L(dve.tensor_scalar(g2[:, :, :], g2[:, :, :], 1.5, -BIG, ALU.is_lt, ALU.mult))
            L(dve.tensor_tensor(g2[:, :, :], g2[:, :, :], g1[:, :, :], ALU.add))
            L(dve.tensor_reduce(gs[:, :, :], by_group(tb), AX.X, ALU.max))
            L(dve.tensor_tensor(gs[:, :, :], gs[:, :, :], g2[:, :, :], ALU.max))
            L(dve.tensor_tensor(gs[:, :, :], gs[:, :, :], g1[:, :, :], ALU.add))
            for g in range(EGRP):
                own = gs[:, :, g:g + 1].broadcast_to([P, NT, EGRP])
                dve.tensor_tensor(pa[:, :, g, :], gs[:, :, :], own, ALU.is_ge)
                last = dve.tensor_tensor(pb[:, :, g, :], gs[:, :, :], own, ALU.is_gt)
            L(last)
            for g in range(EGRP):
                last = dve.tensor_tensor(pa[:, :, g, :], pa[:, :, g, :],
                                         c["lower"][:, g * EGRP:(g + 1) * EGRP][:, None, :].broadcast_to([P, NT, EGRP]), ALU.mult)
            L(last)
            L(dve.tensor_tensor(pa[:, :, :, :].rearrange("p t a b -> p (t a b)"), pa[:, :, :, :].rearrange("p t a b -> p (t a b)"),
                                pb[:, :, :, :].rearrange("p t a b -> p (t a b)"), ALU.max))
            L(dve.tensor_reduce(g1[:, :, :], pa[:, :, :, :], AX.X, ALU.add))
            L(dve.tensor_scalar(g1[:, :, :], g1[:, :, :], TOPG - 0.5, None, ALU.is_lt))
            for g in range(EGRP):
                last = dve.tensor_tensor(ta[:, :, g * EPG:(g + 1) * EPG], ch_[:, :, g * EPG:(g + 1) * EPG],
                                         g1[:, :, g:g + 1].broadcast_to([P, NT, EPG]), ALU.mult)
            L(last)
            L(dve.tensor_scalar(ta[:, :, :], ta[:, :, :], 0.0, None, ALU.add))
            for t in range(NT):
                last = dve.max(top[:, t, :], ta[:, t, :])
            L(last)
            for t in range(NT):
                last = dve.match_replace(tb[:, t, :], top[:, t, :], ta[:, t, :], -BIG)
            L(last)
            L(dve.tensor_scalar(tb[:, :, :], tb[:, :, :], -0.5 * BIG, None, ALU.is_lt))
            L(dve.tensor_tensor(ta[:, :, :], sc[:, :, :], tb[:, :, :], ALU.mult))
            L(dve.tensor_reduce(tot[:, :], ta[:, :, :], AX.X, ALU.add))
            L(dve.tensor_scalar(tot[:, :], tot[:, :], 1e-20, None, ALU.add))
            L(dve.reciprocal(tot[:, :], tot[:, :]))
            L(dve.tensor_tensor(ta[:, :, :], ta[:, :, :], tot[:, :][:, :, None].broadcast_to([P, NT, NEXP]), ALU.mult))
            L(dve.tensor_scalar(ta[:, :, :], ta[:, :, :], ROUTED / WSCALE, None, ALU.mult))
            L(dve.tensor_copy(w3[:, :, 0:NEXP], ta[:, :, :]))
            L(dve.tensor_tensor(tb[:, :, :], ta[:, :, :], w3[:, :, 0:NEXP], ALU.subtract))
            L(dve.tensor_copy(w3[:, :, NEXP:2 * NEXP], tb[:, :, :]))
            dve.tensor_tensor(w3[:, :, 2 * NEXP:3 * NEXP], tb[:, :, :], w3[:, :, NEXP:2 * NEXP], ALU.subtract).then_inc(w3_ready, 1)

        @block.tensor
        def _(pe):
            m.start(pe, "pe")
            pe.wait_ge(w3_ready, ONE + 1)
            with pe.Fori(0, NBLK // 2) as pair:
                k = pair * 2
                for u in range(2):
                    pe.wait_ge(pt_read, ONE + k + u)
                    for j in range(TB):
                        last = pe.matmul(pt[0:3 * NEXP, u, j * P:(j + 1) * P], tile_at(w3, k * TB + (u * TB + j)), c["identb"][:, :],
                                         start=(j == 0), stop=True, skip_group_check=True)
                    last.then_inc(pt_ready, 1)

        @block.scalar
        def _(act):
            m.start(act, "act")
            with act.Fori(0, NBLK // 2) as pair:
                k = pair * 2
                for u in range(2):
                    act.wait_ge(pt_ready, ONE + k + u + 1)
                    act.activation(wT[0:3 * NEXP, bass.ds(k * BLK + u * BLK, BLK)], pt[0:3 * NEXP, u, :], ACT.Copy).then_inc(pt_read, 1)


def experts(nc, stage, c, x, xnT, wT):
    UNITS = 2 * NU
    with Mem(nc, stage) as m:
        gate, up, wide = m.ps("gate", [P, 2, BLK]), m.ps("up", [P, 2, BLK]), m.ps("wide", [P, 2, BLK])
        down = m.ps("down", [P, BLK])
        back = m.ps("back", [P, BLK])
        sg, h1, h2 = m.sb("sg", [P, 2, BLK]), m.sb("h1", [P, BLK]), m.sb("h2", [P, 2, BLK])
        h_parts = m.sb("h_parts", [P, 2, 2, BLK], F16)
        dT = m.sb("dT", [P, BLK])
        gate_ready, up_ready, sg_ready, h_ready = m.sem("gate_ready", "pe"), m.sem("up_ready", "pe"), m.sem("sg_ready", "act"), m.sem("h_ready", "dve", 1)
        high_ready, low_ready, down_done = m.sem("high_ready", "act"), m.sem("low_ready", "dve", 1), m.sem("down_done", "pe", 1)
        dT_ready, back_ready, added, chain = m.sem("dT_ready", "act"), m.sem("back_ready", "pe"), m.sem("added", "dve"), m.sem("chain", "dve")
        block = m.ctx.enter_context(nc.Block())

        @block.tensor
        def _(pe):
            m.start(pe, "pe")

            def gate_and_up(k, unit, g):
                i, at = g % NU, bass.ds(k * BLK, BLK)
                xh, xl = xnT[:, 0, at], xnT[:, 1, at]
                pe.wait_ge(h_ready, ONE + unit)
                product(pe, gate[:, g % 2, :], c["gate_parts"], i, xh, xl).then_inc(gate_ready, 1)
                last = product(pe, up[:, g % 2, :], c["up_parts"], i, xh, xl)
                if i < NPAIR:
                    last = pe.matmul(wide[:, g % 2, :], c["pair_rows"][0:3 * NEXP, i, :], wT[0:3 * NEXP, at], start=True, stop=True)
                last.then_inc(up_ready, 1)

            def down_of(k, unit, g):
                i = g % NU
                pe.wait_ge(low_ready, ONE + unit + 2)
                if i == 0:
                    pe.wait_ge(dT_ready, ONE + k)
                product(pe, down[:, :], c["down_parts"], i, h_parts[:, g % 2, 0, :], h_parts[:, g % 2, 1, :],
                        start=(i == 0), stop=(i == NPAIR)).then_inc(down_done, 1)

            def turn_back(k):
                pe.wait_ge(dT_ready, ONE + k + 1)
                pe.wait_ge(added, ONE + k)
                for j in range(TB):
                    last = pe.transpose(back[:, j * P:(j + 1) * P], dT[:, j * P:(j + 1) * P], c["ident"][:, :])
                last.then_inc(back_ready, 1)

            with pe.Fori(0, NBLK // 2) as pair:
                k, unit = pair * 2, pair * UNITS
                for g in range(UNITS + 3):
                    if g < UNITS:
                        gate_and_up(k + g // NU, unit + g, g)
                    if 2 <= g < UNITS + 2:
                        down_of(k + (g - 2) // NU, unit + (g - 2), g - 2)
                    if g - 2 in (NU, UNITS):
                        turn_back(k + ((g - 2) // NU - 1))

        @block.scalar
        def _(act):
            m.start(act, "act")
            act.preload_act_table_set("silu_and_others")
            with act.Fori(0, NBLK // 2) as pair:
                k, unit = pair * 2, pair * UNITS
                for g in range(UNITS + 2):
                    if g < UNITS:
                        act.wait_ge(gate_ready, ONE + unit + (g + 1))
                        act.wait_ge(h_ready, ONE + unit + g)
                        act.activation(sg[:, g % 2, :], gate[:, g % 2, :], ACT.Silu, scale=1 / WSCALE).then_inc(sg_ready, 1)
                    if 1 <= g < UNITS + 1:
                        act.wait_ge(h_ready, ONE + unit + (g + 1))
                        act.wait_ge(down_done, ONE + unit + (g - 1))
                        act.activation(h_parts[:, (g - 1) % 2, 0, :], h2[:, (g - 1) % 2, :], ACT.Copy).then_inc(high_ready, 1)
                    if g - 1 in (NU, UNITS):
                        done = (g - 1) // NU
                        act.wait_ge(down_done, ONE + unit + (done * NU + 1))
                        act.wait_ge(back_ready, ONE + k + (done - 1))
                        act.activation(dT[:, :], down[:, :], ACT.Copy, scale=1 / WSCALE).then_inc(dT_ready, 1)

        @block.vector
        def _(dve):
            m.start(dve, "dve")

            def hidden(links, unit, g):
                ch = Chain(dve, chain, links)
                dve.wait_ge(sg_ready, ONE + unit + 1)
                dve.wait_ge(up_ready, ONE + unit + 1)
                dve.wait_ge(low_ready, ONE + unit)
                sgu, upu, h = sg[:, g % 2, :], up[:, g % 2, :], h2[:, g % 2, :]
                if g % NU < NPAIR:
                    dve.wait_ge(h_ready, ONE + unit + 1)
                    ch.link(dve.tensor_tensor(h1[:, :], sgu, upu, ALU.mult))
                    dve.tensor_tensor(h, h1[:, :], wide[:, g % 2, :], ALU.mult).then_inc(h_ready, 1)
                else:
                    dve.scalar_tensor_tensor(h, sgu, 1 / WSCALE, upu, ALU.mult, ALU.mult).then_inc(h_ready, 1)

            def low_part(unit, g):
                dve.wait_ge(high_ready, ONE + unit + 1)
                dve.wait_ge(down_done, ONE + unit)
                dve.tensor_tensor(h_parts[:, g % 2, 1, :], h2[:, g % 2, :], h_parts[:, g % 2, 0, :], ALU.subtract).then_inc(low_ready, 1)

            with dve.Fori(0, NBLK // 2) as pair:
                k, unit = pair * 2, pair * UNITS
                for g in range(UNITS + 4):
                    if g < UNITS:
                        hidden(pair * (2 * NPAIR) + (g - g // NU), unit + g, g)
                    if 1 <= g < UNITS + 1:
                        low_part(unit + (g - 1), g - 1)
                    if g - 3 in (NU, UNITS):
                        done = k + ((g - 3) // NU - 1)
                        dve.wait_ge(back_ready, ONE + done + 1)
                        xt = x[:, bass.ds(done * TB, TB), :]
                        dve.tensor_tensor(xt, xt, back[:, :].rearrange("p (t e) -> p t e", t=TB), ALU.add).then_inc(added, 1)


def store_x(nc, x, out):
    with Mem(nc, "store") as m:
        stored = m.sem("stored")
        block = m.ctx.enter_context(nc.Block())

        @block.sync
        def _(sp):
            sp.dma_start(out.rearrange("b (t p) e -> p (b t) e", p=P), x[:, :, :]).then_inc(stored, 16)
            sp.wait_ge(stored, 16)


SHAPES = {
    "ident": ([P, P], F32), "identb": ([P, P], BF16), "ones": ([1, P], F32), "ones2": ([2, BLK], F16), "bias_rows": ([2, 1], F32),
    "band": ([QT, NQT + 1, KW], BF16), "pair_rows": ([3 * NEXP, NPAIR, P], BF16),
    "low_q": ([P, 1], F32), "low_k": ([P, 1], F32), "head_rows": ([P, GH], F32), "lower": ([P, EGRP * EGRP], F32),
    "gate_w": ([E, NEXP], F32), "gate_bias": ([P, NEXP], F32),
}
for _a in ("a_", "b_"):
    SHAPES.update({_a + "WoT": ([E, E], F32), _a + "bv": ([P, E], F32), _a + "bo": ([1, E], F32)})
WEIGHTS = {
    "a_parts": (2 * NG + 1, ASCALE, (("a_WqR", 0), ("a_WkR", NG), ("a_WvT", 2 * NG))),
    "b_parts": (2 * NG + 1, ASCALE, (("b_WqR", 0), ("b_WkR", NG), ("b_WvT", 2 * NG))),
    "gate_parts": (NU, WSCALE, (("Wg", 0), ("Sg", NPAIR))),
    "up_parts": (NU, WSCALE, (("Wu", 0), ("Su", NPAIR))),
    "down_parts": (NU, WSCALE, (("Wd", 0), ("Sd", NPAIR))),
}
ROWS = ("gate_bias", "a_bv", "b_bv")


def build(nc, drams, x_dram, out):
    with ExitStack() as ctx:
        c = {n: ctx.enter_context(nc.sbuf_tensor(f"c_{n}", s, dt)) for n, (s, dt) in SHAPES.items()}
        x = ctx.enter_context(nc.sbuf_tensor("x_tokens", [P, NT, E], F32))
        pairs = []
        for n in SHAPES:
            dst = c[n][tuple(slice(None) for _ in SHAPES[n][0])]
            pairs.append((dst, drams[n].partition_broadcast(P) if n in ROWS else drams[n]))
        for n in WEIGHTS:
            c[n] = ctx.enter_context(nc.sbuf_tensor(f"c_{n}", [P, WEIGHTS[n][0], 2, P], F16))
        c["bias_parts"] = ctx.enter_context(nc.sbuf_tensor("c_bias_parts", [2, 2, 2 * NG, P], F16))
        weights = [(c[n], scale, [(u, drams[src]) for src, u in srcs]) for n, (_, scale, srcs) in WEIGHTS.items()]

        def ffn(name):
            with Mem(nc, name) as m:
                xnT = m.sb("xnT", [P, 2, T], F16)
                sc = m.sb("scores", [P, NT, NEXP])
                wT = m.sb("wT", [3 * NEXP, T], BF16)
                layernorm_transposed(nc, name + "_ln", c, x, xnT, scores=sc)
                route(nc, name + "_route", c, sc, wT)
                experts(nc, name + "_exp", c, x, xnT, wT)

        with Mem(nc, "att_a") as m:
            xnT = m.sb("xnT", [P, 2, T - S + (NQT - 1) * QT + KW], F16)
            with Mem(nc, "load") as early:
                w = Weights(early, weights, [drams["a_bR"], drams["b_bR"]])
                load_all(nc, early, w, pairs, x, x_dram)
                layernorm_transposed(nc, "att_a_ln", c, x, xnT, LEFT)
                split_weights(nc, early, c, w, pairs)
            banded_attention(nc, c, x, xnT)
        ffn("ffn1")
        with Mem(nc, "att_b") as m:
            xnT = m.sb("xnT", [P, 2, T], F16)
            layernorm_transposed(nc, "att_b_ln", c, x, xnT)
            head_softmax_attention(nc, c, x, xnT)
        ffn("ffn2")
        store_x(nc, x, out)


def constants(bf16):
    k = {}
    k["ident"] = np.eye(P, dtype=np.float32)
    k["identb"] = np.eye(P, dtype=np.float32).astype(bf16)
    k["ones"] = np.ones((1, P), np.float32)
    k["ones2"] = np.ones((2, BLK), np.float16)
    k["bias_rows"] = np.array([[0.0], [-1.0]], np.float32)
    band = np.zeros((QT, NQT + 1, KW), np.float32)
    for t in range(NQT):
        q = t * QT + np.arange(QT)[:, None]
        key = t * QT - LEFT + np.arange(KW)[None, :]
        start = q // CHUNK * CHUNK
        ok = (key >= q - LEFT) & (key < start + CHUNK) & (key >= 0) & (key < S)
        ok |= (q >= S)
        band[:, t, :] = np.where(ok, 0.0, -BIG)
    k["band"] = band.astype(bf16)
    rows = np.zeros((3 * NEXP, NPAIR, P), np.float32)
    for part in range(3):
        for i in range(NPAIR):
            for e in range(2):
                rows[part * NEXP + 2 * i + e, i, e * INTER:(e + 1) * INTER] = 1.0
    k["pair_rows"] = rows.astype(bf16)
    part = np.arange(P) // D % 4
    k["low_q"] = np.where(part == 2, -1.0, 0.0).astype(np.float32)[:, None]
    k["low_k"] = np.where(part == 1, -1.0, 0.0).astype(np.float32)[:, None]
    k["head_rows"] = (np.arange(P)[:, None] // 32 == np.arange(GH)[None, :]).astype(np.float32)
    low = (np.arange(EGRP)[None, :] < np.arange(EGRP)[:, None]).astype(np.float32).reshape(1, -1)
    k["lower"] = np.repeat(low, P, axis=0)
    return k


def by_parts(w):
    w = w.reshape((NG, GH, 1, D) + w.shape[1:])
    out = np.zeros((NG, GH, 4, D) + w.shape[4:], w.dtype)
    out[:, :, 0:3] = w
    return out.reshape((NG, P) + w.shape[4:])


def kernel(**inputs):
    import ml_dtypes
    import concourse.bacc as _bacc
    from concourse.bass_utils import run_bass_kernel_spmd as _run

    a = {n: np.asarray(v) for n, v in inputs.items()}
    d = constants(ml_dtypes.bfloat16)
    for s, pre in (("a_", "L0_attn_a_"), ("b_", "L0_attn_b_")):
        for w in "qk":
            d[f"{s}W{w}R"] = by_parts(a[f"{pre}W{w}"]).transpose(2, 0, 1)
        d[s + "bR"] = np.concatenate([by_parts(a[f"{pre}b{w}"]) for w in "qk"])
        d[s + "WvT"] = a[pre + "Wv"].T[:, None, :]
        d[s + "WoT"] = a[pre + "Wo"].T
        d[s + "bv"] = a[pre + "bv"]
        d[s + "bo"] = a[pre + "bo"][None, :]
    f = "L0_ffn_"
    d["gate_w"] = a[f + "gate_w"].T
    d["gate_bias"] = a[f + "gate_bias"]
    d["Wg"] = a[f + "expert_gate"].transpose(2, 0, 1).reshape(E, NPAIR, P)
    d["Wu"] = a[f + "expert_up"].transpose(2, 0, 1).reshape(E, NPAIR, P)
    d["Wd"] = a[f + "expert_down"].transpose(0, 2, 1).reshape(NPAIR, P, E).transpose(1, 0, 2)
    d["Sg"] = a[f + "shared_gate"].T[:, None, :]
    d["Su"] = a[f + "shared_up"].T[:, None, :]
    d["Sd"] = a[f + "shared_down"].T[:, None, :]
    x = np.ascontiguousarray(a["L0_attn_a_hidden_states"])

    nc = _bacc.Bacc("TRN2", target_bir_lowering=False, num_devices=1)
    arrays, drams = {}, {}
    for n in d:
        v = np.ascontiguousarray(d[n])
        arrays["in_" + n] = v
        drams[n] = nc.dram_tensor("in_" + n, v.shape, mybir.dt.from_np(v.dtype), kind="ExternalInput").ap()
    arrays["in_x"] = x
    x_dram = nc.dram_tensor("in_x", x.shape, F32, kind="ExternalInput").ap()
    out = nc.dram_tensor("out_x", x.shape, F32, kind="ExternalOutput").ap()
    build(nc, drams, x_dram, out)
    r = _run(nc, [arrays], core_ids=[0])
    return r.results[0]["out_x"]
```
